# Optimizing a Trainium2 kernel written in Bass

```python
import numpy as np
import jax
import jax.numpy as jnp

def _softmax(x, axis=-1):
    return jax.nn.softmax(x, axis=axis)

def _gelu(x):
    return jax.nn.gelu(x, approximate=True)

def _silu(x):
    return jax.nn.silu(x)

def _sigmoid(x):
    return jax.nn.sigmoid(x)

def _layernorm(x, axis=-1, eps=1e-05):
    m = jnp.mean(x, axis=axis, keepdims=True)
    v = jnp.var(x, axis=axis, keepdims=True)
    return (x - m) / jnp.sqrt(v + eps)

def _scatter_add(tgt, idx, src, axis=0):
    return tgt.at[idx].add(src)

def _segment_sum(src, seg, n):
    return jax.ops.segment_sum(src, seg, n)
kernel_name = 'mk_xattn_ffn_d1_seqx_r8_d7888c'

def setup_inputs(seed: int=0):
    np.random.seed(seed)
    _w = jnp.asarray

    def _rec_inputs():
        import jax
        import jax.numpy as jnp
        _rk = jax.random.key(seed)
        x = -9.806e-05 + 1 * jax.random.normal(jax.random.fold_in(_rk, 1), (4, 512, 128), jnp.float32)
        _lenS = 512 - jax.random.randint(jax.random.fold_in(_rk, 7), (4,), 0, max(1, 512 // 4) + 1, jnp.int32)
        _lenS2 = 32 - jax.random.randint(jax.random.fold_in(_rk, 8), (4,), 0, max(1, 32 // 4) + 1, jnp.int32)
        _ctx_1024P = jax.random.normal(jax.random.fold_in(_rk, 11), (4, 16, 128), jnp.float32)
        _ctx_1024c = jax.random.dirichlet(jax.random.fold_in(_rk, 511), 0.3 * jnp.ones((16,), jnp.float32), (4, 32))
        _ctx_1024t = jnp.einsum('bsk,bkd->bsd', _ctx_1024c, _ctx_1024P)
        _ctx_1024t = _ctx_1024t * jax.lax.rsqrt(jnp.mean(jnp.square(_ctx_1024t)) + 1e-12) * 0.953939
        ctx_1024 = -1.52775e-05 + 0.999936 * (_ctx_1024t + 0.3 * jax.random.normal(jax.random.fold_in(_rk, 611), (4, 32, 128), jnp.float32))
        return (x, ctx_1024)
    x, ctx_1024 = _rec_inputs()

    def _L0_xattn_setup():
        import jax, jax.numpy as jnp
        import numpy as np
        D = 128
        NUM_ITERS = 3
        EPS = 1e-06
        SCALE = D ** (-0.5)

        def rmsnorm(x, w, eps=EPS):
            return x * jax.lax.rsqrt(jnp.mean(x * x, axis=-1, keepdims=True) + eps) * w

        def gru_cell(x, h, wih, whh, bih, bhh):
            gx = x @ wih.T + bih
            gh = h @ whh.T + bhh
            xr, xz, xn = jnp.split(gx, 3, axis=-1)
            hr, hz, hn = jnp.split(gh, 3, axis=-1)
            r = jax.nn.sigmoid(xr + hr)
            z = jax.nn.sigmoid(xz + hz)
            n = jnp.tanh(xn + r * hn)
            return (1.0 - z) * n + z * h
        key = jax.random.key(seed)
        ks = jax.random.split(key, 8)
        B, K, M, d = (8, 64, 512, D)
        w_std = d ** (-0.5)
        return {'slots': jax.random.normal(ks[0], (B, K, d), jnp.float32), 'P': jax.random.normal(ks[1], (B, M, d), jnp.float32), 'Wq': jax.random.normal(ks[2], (d, d), jnp.float32) * w_std, 'Wk': jax.random.normal(ks[3], (d, d), jnp.float32) * w_std, 'Wv': jax.random.normal(ks[4], (d, d), jnp.float32) * w_std, 'gru_wih': jax.random.normal(ks[5], (3 * d, d), jnp.float32) * w_std, 'gru_whh': jax.random.normal(ks[6], (3 * d, d), jnp.float32) * w_std, 'gru_bih': jnp.zeros((3 * d,), jnp.float32), 'gru_bhh': jnp.zeros((3 * d,), jnp.float32), 'slot_norm_w': jnp.ones((d,), jnp.float32), 'input_norm_w': jnp.ones((d,), jnp.float32)}
    _L0_xattn_all = _L0_xattn_setup()
    _L0_xattn_in = {k: v for k, v in _L0_xattn_all.items() if k in ('Wq', 'Wk', 'Wv', 'gru_wih', 'gru_whh', 'gru_bih', 'gru_bhh', 'slot_norm_w', 'input_norm_w')}
    del _L0_xattn_all

    def _L0_ffn_setup():
        import jax, jax.numpy as jnp
        import numpy as np
        CAPACITY_FACTOR = 1.0

        def _route(token_inputs, Wg, capacity):
            dt = token_inputs.dtype
            logits = jnp.einsum('bnd,de->bne', token_inputs, Wg)
            gates = jax.nn.softmax(logits, axis=-1)
            expert_idx = jnp.argmax(gates, axis=-1)
            mask = jax.nn.one_hot(expert_idx, Wg.shape[1], dtype=dt)
            gate = jnp.sum(gates * mask, axis=-1)
            pos = jnp.cumsum(mask, axis=1) * mask - mask
            keep = mask * (pos < capacity).astype(dt)
            pos_oh = jax.nn.one_hot(pos.astype(jnp.int32), capacity, dtype=dt)
            dispatch = keep[..., None] * pos_oh
            combine = dispatch * gate[:, :, None, None]
            return (dispatch, combine)
        key = jax.random.key(seed)
        k1, k2, k3, k4 = jax.random.split(key, 4)
        B, N, D, E, H = (8, 256, 128, 8, 512)
        return {'token_inputs': jax.random.normal(k1, (B, N, D), dtype=jnp.float32), 'Wg': jax.random.normal(k2, (D, E), dtype=jnp.float32) * 0.02, 'W1': jax.random.normal(k3, (E, D, H), dtype=jnp.float32) * 0.02, 'W2': jax.random.normal(k4, (E, H, D), dtype=jnp.float32) * 0.02}
    _L0_ffn_all = _L0_ffn_setup()
    _L0_ffn_in = {k: v for k, v in _L0_ffn_all.items() if k in ('Wg', 'W1', 'W2')}
    del _L0_ffn_all
    return {'x': x, 'ctx_1024': ctx_1024, 'L0_xattn_Wq': _L0_xattn_in['Wq'], 'L0_xattn_Wk': _L0_xattn_in['Wk'], 'L0_xattn_Wv': _L0_xattn_in['Wv'], 'L0_xattn_gru_wih': _L0_xattn_in['gru_wih'], 'L0_xattn_gru_whh': _L0_xattn_in['gru_whh'], 'L0_xattn_gru_bih': _L0_xattn_in['gru_bih'], 'L0_xattn_gru_bhh': _L0_xattn_in['gru_bhh'], 'L0_xattn_slot_norm_w': _L0_xattn_in['slot_norm_w'], 'L0_xattn_input_norm_w': _L0_xattn_in['input_norm_w'], 'L0_ffn_Wg': _L0_ffn_in['Wg'], 'L0_ffn_W1': _L0_ffn_in['W1'], 'L0_ffn_W2': _L0_ffn_in['W2']}

def reference(x, ctx_1024, L0_xattn_Wq, L0_xattn_Wk, L0_xattn_Wv, L0_xattn_gru_wih, L0_xattn_gru_whh, L0_xattn_gru_bih, L0_xattn_gru_bhh, L0_xattn_slot_norm_w, L0_xattn_input_norm_w, L0_ffn_Wg, L0_ffn_W1, L0_ffn_W2):
    import jax
    import jax.numpy as jnp

    def _L0_xattn_ref(slots, P, Wq, Wk, Wv, gru_wih, gru_whh, gru_bih, gru_bhh, slot_norm_w, input_norm_w):
        import jax, jax.numpy as jnp
        import numpy as np
        D = 128
        NUM_ITERS = 3
        EPS = 1e-06
        SCALE = D ** (-0.5)

        def rmsnorm(x, w, eps=EPS):
            return x * jax.lax.rsqrt(jnp.mean(x * x, axis=-1, keepdims=True) + eps) * w

        def gru_cell(x, h, wih, whh, bih, bhh):
            gx = x @ wih.T + bih
            gh = h @ whh.T + bhh
            xr, xz, xn = jnp.split(gx, 3, axis=-1)
            hr, hz, hn = jnp.split(gh, 3, axis=-1)
            r = jax.nn.sigmoid(xr + hr)
            z = jax.nn.sigmoid(xz + hz)
            n = jnp.tanh(xn + r * hn)
            return (1.0 - z) * n + z * h
        Pn = rmsnorm(P, input_norm_w)
        k_proj = Pn @ Wk.T
        v_proj = Pn @ Wv.T
        for _ in range(NUM_ITERS):
            sn = rmsnorm(slots, slot_norm_w)
            q_proj = sn @ Wq.T
            scores = jnp.einsum('bkd,bmd->bkm', q_proj, k_proj) * SCALE
            attn = jax.nn.softmax(scores, axis=-2)
            attn = attn / (jnp.sum(attn, axis=-1, keepdims=True) + EPS)
            updates = jnp.einsum('bkm,bmd->bkd', attn, v_proj)
            slots = gru_cell(updates, slots, gru_wih, gru_whh, gru_bih, gru_bhh)
        return slots

    def _L0_ffn_ref(token_inputs, Wg, W1, W2):
        import jax, jax.numpy as jnp
        import numpy as np
        CAPACITY_FACTOR = 1.0

        def _route(token_inputs, Wg, capacity):
            dt = token_inputs.dtype
            logits = jnp.einsum('bnd,de->bne', token_inputs, Wg)
            gates = jax.nn.softmax(logits, axis=-1)
            expert_idx = jnp.argmax(gates, axis=-1)
            mask = jax.nn.one_hot(expert_idx, Wg.shape[1], dtype=dt)
            gate = jnp.sum(gates * mask, axis=-1)
            pos = jnp.cumsum(mask, axis=1) * mask - mask
            keep = mask * (pos < capacity).astype(dt)
            pos_oh = jax.nn.one_hot(pos.astype(jnp.int32), capacity, dtype=dt)
            dispatch = keep[..., None] * pos_oh
            combine = dispatch * gate[:, :, None, None]
            return (dispatch, combine)
        B, N, D = token_inputs.shape
        E = Wg.shape[1]
        capacity = int(N * CAPACITY_FACTOR // E)
        dispatch, combine = _route(token_inputs, Wg, capacity)
        expert_inputs = jnp.einsum('bnd,bnec->becd', token_inputs, dispatch)
        h = jax.nn.gelu(jnp.einsum('becd,edh->bech', expert_inputs, W1))
        expert_outputs = jnp.einsum('bech,ehd->becd', h, W2)
        output = jnp.einsum('becd,bnec->bnd', expert_outputs, combine)
        return output
    x = x + _L0_xattn_ref(_layernorm(x, axis=-1), ctx_1024, L0_xattn_Wq, L0_xattn_Wk, L0_xattn_Wv, L0_xattn_gru_wih, L0_xattn_gru_whh, L0_xattn_gru_bih, L0_xattn_gru_bhh, L0_xattn_slot_norm_w, L0_xattn_input_norm_w)
    x = x + _L0_ffn_ref(_layernorm(x, axis=-1), L0_ffn_Wg, L0_ffn_W1, L0_ffn_W2)
    return x

_drawn_inputs = setup_inputs


def setup_inputs(seed=0):
    import zlib

    import numpy as np

    out = dict(_drawn_inputs(seed))
    spreads = {'L0_xattn_gru_bih': (0.0, 0.1),
     'L0_xattn_gru_bhh': (0.0, 0.1),
     'L0_xattn_slot_norm_w': (1.0, 0.6),
     'L0_xattn_input_norm_w': (1.0, 0.2)}
    factors = {'L0_ffn_Wg': 8.0, 'L0_ffn_W1': 8.0, 'L0_ffn_W2': 8.0}
    for name, (base, spread) in spreads.items():
        noise = np.random.default_rng([zlib.crc32(name.encode()), seed]).standard_normal(out[name].shape)
        drawn = base * np.exp(spread * noise) if base else spread * noise
        out[name] = jnp.asarray(drawn.astype(out[name].dtype))
    for name, factor in factors.items():
        out[name] = (out[name] * factor).astype(out[name].dtype)
    return out
```

```python
import concourse.bass as bass
from concourse import mybir
from contextlib import ExitStack


def slot_attention_and_switch_ffn(
    nc: bass.Bass,
    x: bass.AP,
    ctx_in: bass.AP,
    Wq: bass.AP,
    Wk: bass.AP,
    Wv: bass.AP,
    wih: bass.AP,
    whh: bass.AP,
    bih: bass.AP,
    bhh: bass.AP,
    slot_w: bass.AP,
    input_w: bass.AP,
    Wg: bass.AP,
    W1: bass.AP,
    W2: bass.AP,
    out: bass.AP,
):
    f32 = mybir.dt.float32
    f32r = mybir.dt.float32r
    bf16 = mybir.dt.bfloat16
    ALU = mybir.AluOpType
    ACT = mybir.ActivationFunctionType
    AX = mybir.AxisListType.X

    P = 128
    B, N, D = x.shape
    M = ctx_in.shape[1]
    G3 = wih.shape[0]
    E = Wg.shape[1]
    H = W1.shape[2]
    CAP = N // E
    NG = 2
    BG = B // NG
    C = N // P
    CG = BG * C
    J = H // P
    NP = E // 2
    KG = BG * M
    SQ = 32
    NB = N // SQ
    ITERS = 3
    EPS_RMS = 1e-6
    EPS_ATT = 1e-6
    EPS_LN = 1e-5
    SCALE = float(D) ** -0.5
    DROPPED = 1024.0

    ctx = ExitStack()
    with ctx:
        def sb(name, shape, dt=f32):
            return ctx.enter_context(nc.sbuf_tensor(name, shape, dt))

        def sem(name):
            return ctx.enter_context(nc.semaphore(name))

        def sems(name, n):
            return [sem(f"{name}{i}") for i in range(n)]

        x_tok = sb("x_tok", [P, B * C, D])
        xn_tok = sb("xn_tok", [P, B * C, D])
        xT = sb("xT", [P, B, N])
        h = sb("h", [P, B, N])
        h2 = sb("h2", [P, B, N])
        ctx_t = sb("ctx_t", [P, D])
        ctx_n = sb("ctx_n", [P, D])
        ctx_sq = sb("ctx_sq", [P, D])
        Wq_t = sb("Wq_t", [P, D])
        Wk_t = sb("Wk_t", [P, D])
        Wv_t = sb("Wv_t", [P, D])
        wih_t = sb("wih_t", [P, 3, D])
        whh_t = sb("whh_t", [P, 3, D])
        rows = sb("rows", [8, D])
        cols = sb("cols", [P, 8])
        half_b = sb("half_b", [P, 2])
        Wg_t = sb("Wg_t", [P, E])
        Wg_c = sb("Wg_c", [P, E])
        WkvT = sb("WkvT", [P, 2, D])
        wihT = sb("wihT", [P, G3])
        whhT = sb("whhT", [P, G3])
        PnT = sb("PnT", [P, B * M])
        kvT = sb("kvT", [P, 2, B * M])
        Msc = sb("Msc", [P, B * M])
        VW = [sb(f"VW{g}", [KG, G3]) for g in range(NG)]
        W1_t = sb("W1_t", [P, E, H])
        W2_t = sb("W2_t", [P, E, J, D])

        ident = sb("ident", [P, P])
        ident_r = sb("ident_r", [P, P], f32r)
        center = sb("center", [P, P])
        mean_w = sb("mean_w", [P, M])
        block1 = sb("block1", [KG, KG])
        tri = sb("tri", [P, P], bf16)
        ones_b = sb("ones_b", [P, P], bf16)
        slot_iota = sb("slot_iota", [P, N])
        pair_iota = sb("pair_iota", [P, NP])
        rev = sb("rev", [P, CG, E])
        mhalf = sb("mhalf", [P, B * C])

        stats = sb("stats", [P, B * C, 6])
        mv = sb("mv", [P, B * C, 2])
        rstd = sb("rstd", [P, B * C])
        ssq = sb("ssq", [P, 1])
        rho_c = sb("rho_c", [P, 1])

        mse = [sb(f"mse{g}", [KG, NB]) for g in range(NG)]
        rho = [sb(f"rho{g}", [KG, NB]) for g in range(NG)]
        rhoT = [sb(f"rhoT{g}", [KG, N]) for g in range(NG)]
        sc = [sb(f"sc{g}", [KG, N]) for g in range(NG)]
        smax = [sb(f"smax{g}", [KG, 1]) for g in range(NG)]
        nmax = [sb(f"nmax{g}", [KG, 1]) for g in range(NG)]
        esum = [sb(f"esum{g}", [KG, 1]) for g in range(NG)]
        einv = [sb(f"einv{g}", [KG, 1]) for g in range(NG)]
        ex = sc
        dlhs = [sb(f"dlhs{g}", [KG, KG]) for g in range(NG)]
        denc = [sb(f"denc{g}", [KG, NB]) for g in range(NG)]
        deni = [sb(f"deni{g}", [KG, NB]) for g in range(NG)]
        attn = [sb(f"attn{g}", [KG, N]) for g in range(NG)]
        msT = attn

        r_b = sb("r_b", [P, B, N])
        z_b = sb("z_b", [P, B, N])
        q_b = sb("q_b", [P, B, N])
        n_b = sb("n_b", [P, B, N])
        d_b = sb("d_b", [P, B, N])

        lg = sb("lg", [P, B * C, E])
        lmax = sb("lmax", [P, B * C])
        lex = sb("lex", [P, B * C, E])
        lsum = sb("lsum", [P, B * C])
        gate = sb("gate", [P, B * C])
        first = sb("first", [P, B * C, E])
        fmax = sb("fmax", [P, B * C])
        mask = sb("mask", [P, B * C, E], bf16)
        mpos = sb("mpos", [P, B * C, E])
        posr = sb("posr", [P, B * C])
        over = sb("over", [P, B * C])
        slot0 = sb("slot0", [P, B * C])
        slot = sb("slot", [P, B * C])
        slot_r = sb("slot_r", [P, B * C], f32r)
        x_hi = sb("x_hi", [P, B * C, D], f32r)
        x_lo = sb("x_lo", [P, B * C, D], f32r)
        disp = sb("disp", [P, 2, C, N], f32r)
        comb = sb("comb", [P, 2, B, N], f32r)
        y_hi = sb("y_hi", [P, 2, B, D], f32r)
        y_lo = sb("y_lo", [P, 2, B, D], f32r)

        x2_tok = xn_tok
        xln = x_tok
        srow = h2
        hid = [a[:, :, :].rearrange("p b n -> p (b n)").rearrange("p (e j s) -> p e j s", e=2, j=J)
               for a in (r_b, z_b)]
        xe = q_b[:, :, :].rearrange("p b n -> p (b n)").rearrange("p (e b c) -> p e b c", e=E, b=B)
        oT = d_b
        res = h

        bank = [ctx.enter_context(nc.psum_tensor(f"bank{i}", [P, N], f32)) for i in range(8)]
        RB, ZB, HB, XB = ([bank[4 * g + k] for g in range(NG)] for k in range(4))
        tok_bank = [bank[0], bank[1], bank[4], bank[5]]
        row_bank = [bank[2], bank[3], bank[6], bank[7]]
        logit_bank = [bank[2], bank[7]]
        pos_bank = [bank[3], bank[6]]
        hid_bank = [bank[2], bank[3]]
        y_bank = [bank[6], bank[7]]
        back_bank = [bank[2], bank[3], bank[6], bank[7]]

        x_in = sems("x_in", B)
        ctx_in_s, wkv_in, wq_in, wih_in, whh_in = (sem(n) for n in ("ctx_ld", "wkv_ld", "wq_ld", "wih_ld", "whh_ld"))
        rows_in, wg_in = sem("rows_ld"), sem("wg_ld")
        w1_in, w2_in = sem("w1_ld"), sem("w2_ld")
        out_done = sems("out_done", B)
        pool_set, dve_set = sem("pool_set"), sem("dve_set")
        xstat, xmv, xrstd, xnorm, xnT, hinit, xTp, xTc = (
            sem(n) for n in ("xstat", "xmv", "xrstd", "xnorm", "xnT", "hinit", "xTp", "xTc"))
        cssq, crho, cnorm, wtr, wtr_c, kv_p, kv_c, m_p, m_c, vw_p, vw_c = (
            sem(n) for n in ("cssq", "crho", "cnorm", "wtr", "wtr_c", "kv_p", "kv_c", "m_p", "m_c", "vw_p", "vw_c"))
        names = ["h_ready", "sq", "ms", "msT", "mse", "rho", "rhoT", "smax", "nmax", "exp", "einv",
                 "dlhs", "den", "denT", "denc", "deni", "rdT", "attn",
                 "rh", "xn", "zp", "tr", "r", "q", "q2", "tz", "n", "d", "e"]
        S = [{k: sem(f"{k}_{'AB'[g]}") for k in names} for g in range(NG)]
        x2T, x2P, x2st, x2mv, x2rs, x2ln, x2c, xhi, xlo = (
            sem(n) for n in ("x2T", "x2P", "x2st", "x2mv", "x2rs", "x2ln", "x2c", "xhi", "xlo"))
        lgP, lgs, lmx, dl, lx, ls, gt, fi, fm, mk, posP, mp, pr, so, sl, slr = (
            sem(n) for n in ("lgP", "lgs", "lmx", "dl", "lx", "ls", "gt", "fi", "fm", "mk", "posP", "mp",
                             "pr", "so", "sl", "slr"))
        dsp, xeP, xeC, srP, srC, cmb, hidP, hidC, yP, yh, yl, accP, oTs, backP, fin = (
            sem(n) for n in ("dsp", "xeP", "xeC", "srP", "srC", "cmb", "hidP", "hidC", "yP", "yh", "yl",
                             "accP", "oTs", "backP", "fin"))

        block = ctx.enter_context(nc.Block())

        def batch(g, i):
            return BG * g + i

        @block.sync
        def _(sp):
            for b in range(B):
                sp.dma_start(x_tok[:, b * C:(b + 1) * C, :],
                             x[b].rearrange("(c p) d -> p c d", p=P)).then_inc(x_in[b], 16)
            sp.dma_start(W1_t[:, :, :], W1.rearrange("e d h -> d e h")).then_inc(w1_in, 16)
            sp.dma_start(W2_t[:, :, :, :], W2.rearrange("e (j p) d -> p e j d", p=P)).then_inc(w2_in, 16)
            for b in range(B):
                sp.wait_ge(fin, (b + 1) * C)
                sp.dma_start(out[b].rearrange("(c p) d -> p c d", p=P),
                             res[:, b, :].rearrange("p (c d) -> p c d", d=D)).then_inc(out_done[b], 16)
            for b in range(B):
                sp.wait_ge(out_done[b], 16)

        @block.gpsimd
        def _(pool):
            nc.gpsimd.memset(ident[:, :], 0.0).then_inc(pool_set, 1)
            nc.gpsimd.memset(tri[:, :], 1.0).then_inc(pool_set, 1)
            pool.wait_ge(pool_set, 2)
            nc.gpsimd.affine_select(out=ident[:, :], in_=ident[:, :], compare_op=ALU.not_equal, fill=1.0,
                                    base=0, pattern=[[-1, P]], channel_multiplier=1).then_inc(pool_set, 1)
            nc.gpsimd.affine_select(out=tri[:, :], in_=tri[:, :], compare_op=ALU.is_gt, fill=0.0,
                                    base=0, pattern=[[1, P]], channel_multiplier=-1).then_inc(pool_set, 1)
            nc.gpsimd.iota(slot_iota[:, :], [[1, N]], base=0, channel_multiplier=0,
                           allow_small_or_imprecise_dtypes=True).then_inc(pool_set, 1)
            nc.gpsimd.iota(pair_iota[:, :], [[P, NP]], base=0, channel_multiplier=1,
                           allow_small_or_imprecise_dtypes=True).then_inc(pool_set, 1)
            nc.gpsimd.iota(rev[:, :, :], [[0, CG], [-1, E]], base=E, channel_multiplier=0,
                           allow_small_or_imprecise_dtypes=True).then_inc(pool_set, 1)

            def rsqrt(dst, src, eps, wait_sem, wait_val, mid, done, done_val, mh):
                pool.wait_ge(wait_sem, wait_val)
                nc.gpsimd.tensor_scalar(dst, src, eps, None, ALU.add).then_inc(mid, 1)

            pool.wait_ge(dve_set, 5)
            pool.wait_ge(cssq, 1)
            nc.gpsimd.tensor_scalar(rho_c[:, :], ssq[:, :], 1.0 / D, EPS_RMS, ALU.mult, ALU.add).then_inc(crho, 1)
            pool.wait_ge(crho, 1)
            nc.gpsimd.tensor_tensor(rho_c[:, :], rho_c[:, :], mhalf[:, 0:1], ALU.pow).then_inc(crho, 1)
            for b in range(B):
                cs = slice(b * C, (b + 1) * C)
                pool.wait_ge(xmv, (b + 1) * C)
                nc.gpsimd.tensor_scalar(rstd[:, cs], mv[:, cs, 1], 1.0, EPS_LN, ALU.mult, ALU.add).then_inc(xrstd, 1)
                pool.wait_ge(xrstd, 2 * b + 1)
                nc.gpsimd.tensor_tensor(rstd[:, cs], rstd[:, cs], mhalf[:, 0:C], ALU.pow).then_inc(xrstd, 1)

            def rho_step(g, t):
                s = S[g]
                pool.wait_ge(s["msT"], t + 1)
                nc.gpsimd.tensor_scalar(mse[g][:, :], msT[g][:, :].rearrange("p (j q) -> p j q", q=SQ)[:, :, 0],
                                        1.0, EPS_RMS, ALU.mult, ALU.add).then_inc(s["mse"], 1)
                pool.wait_ge(s["mse"], t + 1)
                nc.gpsimd.tensor_tensor(rho[g][:, :], mse[g][:, :], mhalf[0:KG, 0:NB], ALU.pow).then_inc(s["rho"], 1)

            def gru_step(g, i, t):
                s, b, k = S[g], batch(g, i), BG * t + i + 1
                pool.wait_ge(s["tr"], k)
                nc.gpsimd.tensor_scalar(r_b[:, b, :], r_b[:, b, :], 0.5, 0.5, ALU.mult, ALU.add).then_inc(s["r"], 1)
                pool.wait_ge(s["n"], k)
                nc.gpsimd.tensor_tensor(d_b[:, b, :], h[:, b, :], n_b[:, b, :], ALU.subtract).then_inc(s["d"], 1)

            rho_step(0, 0)
            for t in range(ITERS):
                gru_step(0, 0, t)
                rho_step(1, t)
                gru_step(0, 1, t)
                gru_step(1, 0, t)
                if t + 1 < ITERS:
                    rho_step(0, t + 1)
                gru_step(1, 1, t)

            for b in range(B):
                cs = slice(b * C, (b + 1) * C)
                pool.wait_ge(x2mv, (b + 1) * C)
                nc.gpsimd.tensor_scalar(rstd[:, cs], mv[:, cs, 1], 1.0, EPS_LN, ALU.mult, ALU.add).then_inc(x2rs, 1)
                pool.wait_ge(x2rs, 2 * b + 1)
                nc.gpsimd.tensor_tensor(rstd[:, cs], rstd[:, cs], mhalf[:, 0:C], ALU.pow).then_inc(x2rs, 1)
                pool.wait_ge(xhi, b + 1)
                nc.gpsimd.tensor_tensor(x_lo[:, cs, :], xln[:, cs, :], x_hi[:, cs, :].bitcast(f32),
                                        ALU.subtract).then_inc(xlo, 1)

        @block.scalar
        def _(act):
            act.dma_start(ctx_t[:, :], ctx_in.rearrange("b m d -> (b m) d")).then_inc(ctx_in_s, 16)
            act.dma_start(rows[0:3, :], bih.rearrange("(a d) -> a d", d=D)).then_inc(rows_in, 16)
            act.dma_start(rows[3:6, :], bhh.rearrange("(a d) -> a d", d=D)).then_inc(rows_in, 16)
            act.dma_start(rows[6:7, :], slot_w.rearrange("(a d) -> a d", d=D)).then_inc(rows_in, 16)
            act.dma_start(rows[7:8, :], input_w.rearrange("(a d) -> a d", d=D)).then_inc(rows_in, 16)
            act.dma_start(Wk_t[:, :], Wk).then_inc(wkv_in, 16)
            act.dma_start(Wv_t[:, :], Wv).then_inc(wkv_in, 16)
            act.dma_start(Wq_t[:, :], Wq).then_inc(wq_in, 16)
            act.dma_start(whh_t[:, :, :], whh.rearrange("(a p) d -> p a d", p=P)).then_inc(whh_in, 16)
            act.dma_start(wih_t[:, :, :], wih.rearrange("(a p) d -> p a d", p=P)).then_inc(wih_in, 16)
            act.dma_start(Wg_t[:, :], Wg).then_inc(wg_in, 16)

            act.wait_ge(wtr, 2)
            nc.scalar.activation(WkvT[:, :, :], bank[0][:, 0:2 * P].rearrange("p (a d) -> p a d", d=D),
                                 ACT.Copy).then_inc(wtr_c, 1)
            act.wait_ge(wtr, 3)
            nc.scalar.activation(whhT[:, :], bank[2][:, 0:G3], ACT.Copy).then_inc(wtr_c, 1)
            act.wait_ge(wtr, 4)
            nc.scalar.activation(wihT[:, :], bank[1][:, 0:G3], ACT.Copy).then_inc(wtr_c, 1)

            def square(g, i, t):
                s, b = S[g], batch(g, i)
                act.wait_ge(s["h_ready"], BG * t + i + 1)
                nc.scalar.activation(h2[:, b, :], h[:, b, :], ACT.Square).then_inc(s["sq"], 1)

            for b in range(B):
                act.wait_ge(xnT, b + 1)
                nc.scalar.activation(h[:, b, :], bank[4 + b][:, :], ACT.Copy).then_inc(S[b // BG]["h_ready"], 1)
                square(b // BG, b % BG, 0)
            for b in range(B):
                act.wait_ge(xTp, b + 1)
                nc.scalar.activation(xT[:, b, :], bank[4 + b][:, :], ACT.Copy).then_inc(xTc, 1)

            def exps(g, t):
                s = S[g]
                act.wait_ge(s["nmax"], t + 1)
                nc.scalar.activation(ex[g][:, :], sc[g][:, :], ACT.Exp, bias=nmax[g][:, 0:1],
                                     accum_out=esum[g][:, 0:1]).then_inc(s["exp"], 1)

            def reset(g, i, t):
                s, b, k = S[g], batch(g, i), BG * t + i + 1
                act.wait_ge(s["rh"], k)
                nc.scalar.activation(r_b[:, b, :], RB[g][:, :], ACT.Tanh, bias=half_b[:, 0:1],
                                     scale=0.5).then_inc(s["tr"], 1)

            def update(g, i, t):
                s, b, k = S[g], batch(g, i), BG * t + i + 1
                act.wait_ge(s["zp"], k)
                nc.scalar.activation(z_b[:, b, :], ZB[g][:, :], ACT.Tanh, bias=half_b[:, 1:2],
                                     scale=0.5).then_inc(s["tz"], 1)

            def candidate(g, i, t):
                s, b, k = S[g], batch(g, i), BG * t + i + 1
                act.wait_ge(s["q2"], k)
                nc.scalar.activation(n_b[:, b, :], q_b[:, b, :], ACT.Tanh, bias=cols[:, 2:3]).then_inc(s["n"], 1)

            act.wait_ge(m_c, 4)
            exps(0, 0)
            for t in range(ITERS):
                reset(0, 0, t)
                update(0, 0, t)
                candidate(0, 0, t)
                if t + 1 < ITERS:
                    square(0, 0, t + 1)
                reset(0, 1, t)
                exps(1, t)
                update(0, 1, t)
                candidate(0, 1, t)
                if t + 1 < ITERS:
                    square(0, 1, t + 1)
                reset(1, 0, t)
                update(1, 0, t)
                candidate(1, 0, t)
                if t + 1 < ITERS:
                    square(1, 0, t + 1)
                reset(1, 1, t)
                if t + 1 < ITERS:
                    exps(0, t + 1)
                update(1, 1, t)
                candidate(1, 1, t)
                if t + 1 < ITERS:
                    square(1, 1, t + 1)

            for g in range(NG):
                for i in range(BG):
                    b = batch(g, i)
                    cs = slice(b * C, (b + 1) * C)
                    act.wait_ge(x2P, b + 1)
                    nc.scalar.activation(x2_tok[:, cs, :], tok_bank[b][:, :].rearrange("p (c d) -> p c d", d=D),
                                         ACT.Copy).then_inc(x2c, 1)
                    act.wait_ge(x2ln, (b + 1) * C)
                    nc.scalar.activation(x_hi[:, cs, :], xln[:, cs, :], ACT.Copy).then_inc(xhi, 1)
                act.wait_ge(dl, g + 1)
                gs = slice(g * CG, (g + 1) * CG)
                nc.scalar.activation(lex[:, gs, :], lg[:, gs, :], ACT.Exp).then_inc(lx, 1)
            for b in range(B):
                act.wait_ge(xeP, b + 1)
                nc.scalar.activation(xe[:, :, b, :], tok_bank[b][:, :].rearrange("p (e c) -> p e c", c=CAP),
                                     ACT.Copy).then_inc(xeC, 1)
                act.wait_ge(srP, b + 1)
                nc.scalar.activation(srow[:, b, :], row_bank[b][:, :], ACT.Copy).then_inc(srC, 1)

            def gelu(k):
                for e in range(2):
                    for half in range(2):
                        n = (2 * k + e) * 2 + half
                        act.wait_ge(hidP, n + 1)
                        dst = hid[k % 2][:, e, 2 * half:2 * half + 2, :]
                        if k >= 2:
                            act.wait_ge(yP, k - 1)
                        nc.scalar.activation(dst, hid_bank[half][:, :].rearrange("p (a s) -> p a s", s=B * CAP),
                                             ACT.Gelu_apprx_tanh).then_inc(hidC, 1)

            def y_high(k):
                act.wait_ge(yP, k + 1)
                if k >= 2:
                    act.wait_ge(accP, k - 1)
                nc.scalar.activation(y_hi[:, k % 2, :, :], y_bank[k % 2][:, :].rearrange("p (b d) -> p b d", d=D),
                                     ACT.Copy).then_inc(yh, 1)

            gelu(0)
            for k in range(NP):
                if k + 1 < NP:
                    gelu(k + 1)
                y_high(k)
            for b in range(B):
                act.wait_ge(accP, NP - 1 + b + 1)
                nc.scalar.activation(oT[:, b, :], tok_bank[b][:, :], ACT.Copy).then_inc(oTs, 1)

        @block.vector
        def _(dve):
            v = nc.vector
            v.memset(mean_w[:, :], 1.0 / D).then_inc(dve_set, 1)
            v.memset(ones_b[:, :], 1.0).then_inc(dve_set, 1)
            v.memset(block1[:, :], 0.0).then_inc(dve_set, 1)
            dve.wait_ge(dve_set, 3)
            for i in range(BG):
                last = v.memset(block1[i * M:(i + 1) * M, i * M:(i + 1) * M], 1.0)
            last.then_inc(dve_set, 1)
            v.memset(mhalf[:, :], -0.5).then_inc(dve_set, 1)
            dve.wait_ge(pool_set, 4)
            v.tensor_scalar(center[:, :], ident[:, :], -1.0 / D, None, ALU.add).then_inc(dve_set, 1)
            v.tensor_copy(ident_r[:, :], ident[:, :]).then_inc(dve_set, 1)

            dve.wait_ge(ctx_in_s, 16)
            v.tensor_tensor_reduce(out=ctx_sq[:, :], in0=ctx_t[:, :], in1=ctx_t[:, :], scale=1.0, scalar=0.0,
                                   op0=ALU.mult, op1=ALU.add, accum_out=ssq[:, 0:1]).then_inc(cssq, 1)

            def x_stats(b):
                dve.wait_ge(x_in[b], 16)
                for c in range(b * C, (b + 1) * C):
                    v.bn_stats(stats[:, c, :], x_tok[:, c, :]).then_inc(xstat, 1)
                for c in range(b * C, (b + 1) * C):
                    dve.wait_ge(xstat, c + 1)
                    v.bn_aggr(mv[:, c, :], stats[:, c, :]).then_inc(xmv, 1)

            def x_norm(b):
                dve.wait_ge(xrstd, 2 * b + 2)
                for c in range(b * C, (b + 1) * C):
                    v.tensor_scalar(xn_tok[:, c, :], x_tok[:, c, :], mv[:, c, 0:1], rstd[:, c:c + 1],
                                    ALU.subtract, ALU.mult).then_inc(xnorm, 1)

            x_stats(0)
            dve.wait_ge(crho, 2)
            v.tensor_scalar(ctx_n[:, :], ctx_t[:, :], rho_c[:, 0:1], None, ALU.mult).then_inc(cnorm, 1)
            x_stats(1)
            x_norm(0)
            dve.wait_ge(wtr, 1)
            v.tensor_copy(cols[:, :], bank[3][:, 0:8]).then_inc(m_c, 1)
            dve.wait_ge(m_c, 1)
            v.tensor_tensor(half_b[:, :], cols[:, 0:2], cols[:, 3:5], ALU.add).then_inc(m_c, 1)
            dve.wait_ge(wtr, 2)
            v.tensor_scalar(PnT[:, :], bank[3][:, 0:P], cols[:, 7:8], None, ALU.mult).then_inc(m_c, 1)
            dve.wait_ge(m_c, 3)
            v.tensor_scalar(half_b[:, :], half_b[:, :], 0.5, None, ALU.mult).then_inc(m_c, 1)
            x_norm(1)
            dve.wait_ge(kv_p, 1)
            v.tensor_copy(kvT[:, :, :], bank[0][:, 0:2 * B * M].rearrange("p (a m) -> p a m", a=2)).then_inc(kv_c, 1)
            x_stats(2)
            dve.wait_ge(m_p, 1)
            v.tensor_scalar(Msc[:, :], bank[3][:, 0:B * M], cols[:, 6:7], SCALE, ALU.mult, ALU.mult).then_inc(m_c, 1)
            v.tensor_copy(Wg_c[:, :], bank[3][:, 256:256 + E]).then_inc(m_c, 1)
            x_stats(3)
            x_norm(2)
            for g in range(NG):
                dve.wait_ge(vw_p, g + 1)
                v.tensor_copy(VW[g][:, :], bank[1 + g][0:KG, 0:G3]).then_inc(vw_c, 1)
            x_norm(3)

            def scores(g, t):
                s = S[g]
                dve.wait_ge(s["ms"], t + 1)
                v.transpose(msT[g][:, :], HB[g][0:KG, :]).then_inc(s["msT"], 1)
                dve.wait_ge(s["rho"], t + 1)
                v.transpose(rhoT[g][:, :].rearrange("p (j q) -> p j q", q=SQ),
                            rho[g][:, :].unsqueeze(2).broadcast_to([KG, NB, SQ])).then_inc(s["rhoT"], 1)
                dve.wait_ge(s["rhoT"], t + 1)
                v.tensor_tensor_reduce(out=sc[g][:, :], in0=RB[g][0:KG, :], in1=rhoT[g][:, :], scale=1.0,
                                       scalar=-3.0e38, op0=ALU.mult, op1=ALU.max,
                                       accum_out=smax[g][:, 0:1]).then_inc(s["smax"], 1)
                dve.wait_ge(s["smax"], t + 1)
                v.tensor_scalar(nmax[g][:, :], smax[g][:, :], -1.0, None, ALU.mult).then_inc(s["nmax"], 1)

            def softmax_scale(g, t):
                s = S[g]
                dve.wait_ge(s["exp"], t + 1)
                v.reciprocal(einv[g][:, :], esum[g][:, :]).then_inc(s["einv"], 1)
                dve.wait_ge(s["einv"], t + 1)
                v.tensor_scalar(dlhs[g][:, :], block1[:, :], einv[g][:, 0:1], None, ALU.mult).then_inc(s["dlhs"], 1)

            def attention(g, t):
                s = S[g]
                dve.wait_ge(s["den"], t + 1)
                v.transpose(msT[g][:, :], XB[g][0:KG, :]).then_inc(s["denT"], 1)
                dve.wait_ge(s["denT"], t + 1)
                v.tensor_scalar(denc[g][:, :], msT[g][:, :].rearrange("p (j q) -> p j q", q=SQ)[:, :, 0],
                                EPS_ATT, None, ALU.add).then_inc(s["denc"], 1)
                dve.wait_ge(s["denc"], t + 1)
                v.reciprocal(deni[g][:, :], denc[g][:, :]).then_inc(s["deni"], 1)
                dve.wait_ge(s["deni"], t + 1)
                v.transpose(rhoT[g][:, :].rearrange("p (j q) -> p j q", q=SQ),
                            deni[g][:, :].unsqueeze(2).broadcast_to([KG, NB, SQ])).then_inc(s["rdT"], 1)
                dve.wait_ge(s["rdT"], t + 1)
                v.scalar_tensor_tensor(out=attn[g][:, :], in0=ex[g][:, :], scalar=einv[g][:, 0:1],
                                       in1=rhoT[g][:, :], op0=ALU.mult, op1=ALU.mult).then_inc(s["attn"], 1)

            def gru_in(g, i, t):
                s, b, k = S[g], batch(g, i), BG * t + i + 1
                dve.wait_ge(s["r"], k)
                v.scalar_tensor_tensor(out=q_b[:, b, :], in0=HB[g][:, :], scalar=cols[:, 5:6], in1=r_b[:, b, :],
                                       op0=ALU.add, op1=ALU.mult).then_inc(s["q"], 1)
                dve.wait_ge(s["q"], k)
                dve.wait_ge(s["xn"], k)
                v.tensor_tensor(q_b[:, b, :], q_b[:, b, :], XB[g][:, :], ALU.add).then_inc(s["q2"], 1)

            def gru_out(g, i, t):
                s, b, k = S[g], batch(g, i), BG * t + i + 1
                dve.wait_ge(s["tz"], k)
                dve.wait_ge(s["d"], k)
                v.scalar_tensor_tensor(out=d_b[:, b, :], in0=z_b[:, b, :], scalar=1.0, in1=d_b[:, b, :],
                                       op0=ALU.add, op1=ALU.mult).then_inc(s["e"], 1)
                dve.wait_ge(s["e"], k)
                v.scalar_tensor_tensor(out=h[:, b, :], in0=d_b[:, b, :], scalar=0.5, in1=n_b[:, b, :],
                                       op0=ALU.mult, op1=ALU.add).then_inc(s["h_ready"], 1)

            def final_x(g, i):
                b = batch(g, i)
                dve.wait_ge(xTc, b + 1)
                dve.wait_ge(S[g]["h_ready"], BG * ITERS + i + 1)
                v.tensor_tensor(xT[:, b, :], xT[:, b, :], h[:, b, :], ALU.add).then_inc(x2T, 1)

            scores(0, 0)
            softmax_scale(0, 0)
            attention(0, 0)
            for t in range(ITERS):
                gru_in(0, 0, t)
                gru_out(0, 0, t)
                scores(1, t)
                gru_in(0, 1, t)
                softmax_scale(1, t)
                gru_out(0, 1, t)
                attention(1, t)
                if t + 1 == ITERS:
                    final_x(0, 0)
                    final_x(0, 1)
                gru_in(1, 0, t)
                gru_out(1, 0, t)
                if t + 1 < ITERS:
                    scores(0, t + 1)
                gru_in(1, 1, t)
                if t + 1 < ITERS:
                    softmax_scale(0, t + 1)
                gru_out(1, 1, t)
                if t + 1 < ITERS:
                    attention(0, t + 1)
            final_x(1, 0)
            final_x(1, 1)

            def x2_stats(b):
                dve.wait_ge(x2c, b + 1)
                for c in range(b * C, (b + 1) * C):
                    v.bn_stats(stats[:, c, :], x2_tok[:, c, :]).then_inc(x2st, 1)
                for c in range(b * C, (b + 1) * C):
                    dve.wait_ge(x2st, c + 1)
                    v.bn_aggr(mv[:, c, :], stats[:, c, :]).then_inc(x2mv, 1)

            def x2_norm(b):
                dve.wait_ge(x2rs, 2 * b + 2)
                for c in range(b * C, (b + 1) * C):
                    v.tensor_scalar(xln[:, c, :], x2_tok[:, c, :], mv[:, c, 0:1], rstd[:, c:c + 1],
                                    ALU.subtract, ALU.mult).then_inc(x2ln, 1)

            def route(g):
                gs = slice(g * CG, (g + 1) * CG)
                full = [P, CG, E]

                def wide(a):
                    return a[:, gs].unsqueeze(2).broadcast_to(full)
                dve.wait_ge(lgP, g + 1)
                dve.wait_ge(x2rs, 2 * BG * (g + 1))
                v.tensor_tensor(lg[:, gs, :], logit_bank[g][:, 0:CG * E].rearrange("p (c e) -> p c e", e=E),
                                wide(rstd), ALU.mult).then_inc(lgs, 1)
                dve.wait_ge(lgs, g + 1)
                v.reduce_max(lmax[:, gs], lg[:, gs, :], AX).then_inc(lmx, 1)
                dve.wait_ge(lmx, g + 1)
                v.tensor_tensor(lg[:, gs, :], lg[:, gs, :], wide(lmax), ALU.subtract).then_inc(dl, 1)
                dve.wait_ge(dl, g + 1)
                v.scalar_tensor_tensor(out=first[:, gs, :], in0=lg[:, gs, :], scalar=0.0, in1=rev[:, :, :],
                                       op0=ALU.is_ge, op1=ALU.mult).then_inc(fi, 1)
                dve.wait_ge(fi, g + 1)
                v.reduce_max(fmax[:, gs], first[:, gs, :], AX).then_inc(fm, 1)
                dve.wait_ge(fm, g + 1)
                v.tensor_tensor(mask[:, gs, :], first[:, gs, :], wide(fmax), ALU.is_equal).then_inc(mk, 1)
                dve.wait_ge(lx, g + 1)
                v.reduce_sum(lsum[:, gs], lex[:, gs, :], AX).then_inc(ls, 1)
                dve.wait_ge(ls, g + 1)
                v.reciprocal(gate[:, gs], lsum[:, gs]).then_inc(gt, 1)
                dve.wait_ge(posP, g + 1)
                v.tensor_tensor(mpos[:, gs, :], pos_bank[g][:, 0:CG * E].rearrange("p (c e) -> p c e", e=E),
                                mask[:, gs, :], ALU.mult).then_inc(mp, 1)
                dve.wait_ge(mp, g + 1)
                v.reduce_sum(posr[:, gs], mpos[:, gs, :], AX).then_inc(pr, 1)
                dve.wait_ge(pr, g + 1)
                v.tensor_scalar(over[:, gs], posr[:, gs], float(CAP), DROPPED, ALU.is_ge, ALU.mult).then_inc(so, 1)
                v.scalar_tensor_tensor(out=slot0[:, gs], in0=fmax[:, gs], scalar=-float(CAP), in1=posr[:, gs],
                                       op0=ALU.mult, op1=ALU.add).then_inc(so, 1)
                dve.wait_ge(so, 2 * g + 2)
                v.scalar_tensor_tensor(out=slot[:, gs], in0=slot0[:, gs], scalar=float(CAP * E), in1=over[:, gs],
                                       op0=ALU.add, op1=ALU.add).then_inc(sl, 1)
                dve.wait_ge(sl, g + 1)
                v.tensor_copy(slot_r[:, gs], slot[:, gs]).then_inc(slr, 1)

            def dispatch_hot(b):
                for c in range(C):
                    if b >= 2:
                        dve.wait_ge(xeP, b - 1)
                    v.tensor_scalar(disp[:, b % 2, c, :], slot_iota[:, :], slot[:, b * C + c:b * C + c + 1], None,
                                    ALU.is_equal).then_inc(dsp, 1)

            for g in range(NG):
                x2_stats(batch(g, 0))
                x2_norm(batch(g, 0))
                x2_stats(batch(g, 1))
                x2_norm(batch(g, 1))
                route(g)
                dispatch_hot(batch(g, 0))
                dispatch_hot(batch(g, 1))

            def combine_hot(k):
                if k >= 2:
                    dve.wait_ge(accP, k - 1)
                for b in range(B):
                    dve.wait_ge(srC, b + 1)
                    v.tensor_scalar(comb[:, k % 2, b, :], srow[:, b, :], pair_iota[:, k:k + 1], None,
                                    ALU.is_equal).then_inc(cmb, 1)

            def y_low(k):
                dve.wait_ge(yh, k + 1)
                if k >= 2:
                    dve.wait_ge(accP, k - 1)
                v.tensor_tensor(y_lo[:, k % 2, :, :], y_bank[k % 2][:, :].rearrange("p (b d) -> p b d", d=D),
                                y_hi[:, k % 2, :, :].bitcast(f32), ALU.subtract).then_inc(yl, 1)

            for k in range(NP):
                combine_hot(k)
                y_low(k)
            for b in range(B):
                dve.wait_ge(backP, b + 1)
                for c in range(C):
                    n = b * C + c
                    v.scalar_tensor_tensor(out=res[:, b, c * D:(c + 1) * D], in0=back_bank[b][:, c * D:(c + 1) * D],
                                           scalar=gate[:, n:n + 1], in1=x2_tok[:, n, :],
                                           op0=ALU.mult, op1=ALU.add).then_inc(fin, 1)

        @block.tensor
        def _(pe):
            mm = nc.tensor.matmul
            tr = nc.tensor.transpose

            pe.wait_ge(pool_set, 4)
            pe.wait_ge(rows_in, 64)
            tr(bank[3][:, 0:8], rows[:, :], ident[0:8, 0:8]).then_inc(wtr, 1)
            pe.wait_ge(wkv_in, 32)
            tr(bank[0][:, 0:P], Wk_t[:, :], ident[:, :])
            tr(bank[0][:, P:2 * P], Wv_t[:, :], ident[:, :])
            pe.wait_ge(m_c, 1)
            pe.wait_ge(cnorm, 1)
            tr(bank[3][:, 0:P], ctx_n[:, :], ident[:, :]).then_inc(wtr, 1)
            pe.wait_ge(whh_in, 16)
            for a in range(3):
                last = tr(bank[2][:, a * P:(a + 1) * P], whh_t[:, a, :], ident[:, :])
            last.then_inc(wtr, 1)
            pe.wait_ge(wih_in, 16)
            for a in range(3):
                last = tr(bank[1][:, a * P:(a + 1) * P], wih_t[:, a, :], ident[:, :])
            last.then_inc(wtr, 1)

            def norm_T(b):
                pe.wait_ge(xnorm, (b + 1) * C)
                for c in range(C):
                    last = tr(bank[4 + b][:, c * P:(c + 1) * P], xn_tok[:, b * C + c, :], ident[:, :])
                last.then_inc(xnT, 1)

            norm_T(0)
            pe.wait_ge(m_c, 3)
            pe.wait_ge(wtr_c, 1)
            mm(bank[0][:, 0:B * M], WkvT[:, 0, :], PnT[:, :], start=True, stop=True)
            mm(bank[0][:, B * M:2 * B * M], WkvT[:, 1, :], PnT[:, :], start=True, stop=True).then_inc(kv_p, 1)
            norm_T(1)
            pe.wait_ge(wq_in, 16)
            pe.wait_ge(wg_in, 16)
            pe.wait_ge(dve_set, 7)
            pe.wait_ge(kv_c, 1)
            mm(bank[3][:, 0:B * M], Wq_t[:, :], kvT[:, 0, :], start=True, stop=True)
            mm(bank[3][:, 256:256 + E], center[:, :], Wg_t[:, :], start=True, stop=True).then_inc(m_p, 1)
            pe.wait_ge(wtr_c, 3)
            for g in range(NG):
                mm(bank[1 + g][0:KG, 0:G3], kvT[:, 1, g * KG:(g + 1) * KG], wihT[:, :],
                   start=True, stop=True).then_inc(vw_p, 1)
            norm_T(2)
            norm_T(3)

            def scores(g, t):
                s = S[g]
                pe.wait_ge(s["h_ready"], BG * (t + 1))
                for i in range(BG):
                    b = batch(g, i)
                    mm(RB[g][i * M:(i + 1) * M, :], Msc[:, b * M:(b + 1) * M], h[:, b, :], start=True, stop=True)
                pe.wait_ge(s["sq"], BG * (t + 1))
                for i in range(BG):
                    b = batch(g, i)
                    last = mm(HB[g][i * M:(i + 1) * M, :], mean_w[:, :], h2[:, b, :], start=True, stop=True)
                last.then_inc(s["ms"], 1)

            def denominators(g, t):
                s = S[g]
                pe.wait_ge(s["dlhs"], t + 1)
                mm(XB[g][0:KG, :], dlhs[g][:, :], ex[g][:, :], start=True, stop=True).then_inc(s["den"], 1)

            def from_slots(g, i, t):
                s, b = S[g], batch(g, i)
                if i == 0:
                    pe.wait_ge(s["smax"], t + 1)
                else:
                    pe.wait_ge(s["tr"], BG * t + i)
                mm(RB[g][:, :], whhT[:, 0:P], h[:, b, :], start=True, stop=False)
                if i > 0:
                    pe.wait_ge(s["q"], BG * t + i)
                mm(HB[g][:, :], whhT[:, 2 * P:3 * P], h[:, b, :], start=True, stop=True)
                if i > 0:
                    pe.wait_ge(s["tz"], BG * t + i)
                mm(ZB[g][:, :], whhT[:, P:2 * P], h[:, b, :], start=True, stop=False)

            def from_attention(g, i, t):
                s = S[g]
                pe.wait_ge(s["attn"], t + 1)
                w = VW[g][i * M:(i + 1) * M, :]
                a = attn[g][i * M:(i + 1) * M, :]
                mm(RB[g][:, :], w[:, 0:P], a, start=False, stop=True).then_inc(s["rh"], 1)
                if i > 0:
                    pe.wait_ge(s["q2"], BG * t + i)
                mm(XB[g][:, :], w[:, 2 * P:3 * P], a, start=True, stop=True).then_inc(s["xn"], 1)
                mm(ZB[g][:, :], w[:, P:2 * P], a, start=False, stop=True).then_inc(s["zp"], 1)

            def x_T(b):
                pe.wait_ge(S[b // BG]["h_ready"], b % BG + 1)
                for c in range(C):
                    last = tr(bank[4 + b][:, c * P:(c + 1) * P], x_tok[:, b * C + c, :], ident[:, :])
                last.then_inc(xTp, 1)

            def x2_back(b):
                g = b // BG
                pe.wait_ge(x2T, b + 1)
                for c in range(C):
                    last = tr(tok_bank[b][:, c * P:(c + 1) * P], xT[:, b, c * P:(c + 1) * P], ident[:, :])
                last.then_inc(x2P, 1)
                for c in range(C):
                    n = (b % BG) * C + c
                    last = mm(logit_bank[g][:, n * E:(n + 1) * E], xT[:, b, c * P:(c + 1) * P], Wg_c[:, :],
                              start=True, stop=True)
                if b % BG == BG - 1:
                    last.then_inc(lgP, 1)

            pe.wait_ge(m_c, 6)
            pe.wait_ge(vw_c, 2)
            scores(0, 0)
            for b in range(B):
                x_T(b)
            denominators(0, 0)
            for t in range(ITERS):
                from_slots(0, 0, t)
                from_attention(0, 0, t)
                if t == 0:
                    pe.wait_ge(xTc, B)
                scores(1, t)
                from_slots(0, 1, t)
                from_attention(0, 1, t)
                denominators(1, t)
                from_slots(1, 0, t)
                from_attention(1, 0, t)
                if t + 1 < ITERS:
                    scores(0, t + 1)
                else:
                    x2_back(0)
                    x2_back(1)
                from_slots(1, 1, t)
                from_attention(1, 1, t)
                if t + 1 < ITERS:
                    denominators(0, t + 1)
            x2_back(2)
            x2_back(3)

            def positions(g):
                pe.wait_ge(mk, g + 1)
                m4 = mask[:, g * CG:(g + 1) * CG, :].rearrange("p (b c) e -> p b c e", c=C)
                o4 = pos_bank[g][:, 0:CG * E].rearrange("p (b c e) -> p b c e", c=C, e=E)
                for i in range(BG):
                    for k in range(1, C):
                        mm(o4[:, i, k:C, :].rearrange("p c e -> p (c e)"), ones_b[:, :],
                           m4[:, i, 0:C - k, :].rearrange("p c e -> p (c e)"), start=(i == 0 and k == 1),
                           stop=False, skip_group_check=True)
                last = mm(pos_bank[g][:, 0:CG * E], tri[:, :],
                          mask[:, g * CG:(g + 1) * CG, :].rearrange("p c e -> p (c e)"),
                          start=False, stop=True, skip_group_check=True)
                last.then_inc(posP, 1)

            def slot_rows(b):
                pe.wait_ge(slr, b // BG + 1)
                for c in range(C):
                    last = mm(row_bank[b][:, c * P:(c + 1) * P], slot_r[:, b * C + c:b * C + c + 1].broadcast_to([P, P]),
                              ident_r[:, :], start=True, stop=True)
                last.then_inc(srP, 1)

            def dispatch(b):
                pe.wait_ge(xlo, b + 1)
                pe.wait_ge(x2ln, (b + 1) * C)
                for c in range(C):
                    pe.wait_ge(dsp, b * C + c + 1)
                    for part in (x_hi, x_lo):
                        last = mm(tok_bank[b][:, :], part[:, b * C + c, :], disp[:, b % 2, c, :],
                                  start=(c == 0 and part is x_hi), stop=(c == C - 1 and part is x_lo))
                last.then_inc(xeP, 1)

            for g in range(NG):
                positions(g)
                for i in range(BG):
                    dispatch(batch(g, i))
                for i in range(BG):
                    slot_rows(batch(g, i))

            def up(k):
                for e in range(2):
                    ex_ = 2 * k + e
                    rhs = xe[:, ex_, :, :].rearrange("p b c -> p (b c)")
                    for half in range(2):
                        n = 2 * ex_ + half
                        if n >= 2:
                            pe.wait_ge(hidC, n - 1)
                        for a in range(2):
                            j = 2 * half + a
                            last = mm(hid_bank[half][:, a * B * CAP:(a + 1) * B * CAP],
                                      W1_t[:, ex_, j * P:(j + 1) * P], rhs, start=True, stop=True)
                        last.then_inc(hidP, 1)

            def down(k):
                pe.wait_ge(hidC, 4 * (k + 1))
                if k >= 2:
                    pe.wait_ge(yl, k - 1)
                for b in range(B):
                    for j in range(J):
                        for e in range(2):
                            last = mm(y_bank[k % 2][e * CAP:(e + 1) * CAP, b * D:(b + 1) * D],
                                      hid[k % 2][:, e, j, b * CAP:(b + 1) * CAP], W2_t[:, 2 * k + e, j, :],
                                      start=(j == 0), stop=(j == J - 1))
                last.then_inc(yP, 1)

            def combine(k):
                pe.wait_ge(yl, k + 1)
                pe.wait_ge(cmb, (k + 1) * B)
                for b in range(B):
                    for part in (y_hi, y_lo):
                        last = mm(tok_bank[b][:, :], part[:, k % 2, b, :], comb[:, k % 2, b, :],
                                  start=(k == 0 and part is y_hi), stop=(k == NP - 1 and part is y_lo))
                    if k == NP - 1 or b == B - 1:
                        last.then_inc(accP, 1)

            pe.wait_ge(w1_in, 16)
            pe.wait_ge(w2_in, 16)
            pe.wait_ge(xeC, B)
            pe.wait_ge(srC, B)
            up(0)
            for k in range(NP):
                if k + 1 < NP:
                    up(k + 1)
                down(k)
                if k > 0:
                    combine(k - 1)
            combine(NP - 1)
            for b in range(B):
                pe.wait_ge(oTs, b + 1)
                for c in range(C):
                    last = tr(back_bank[b][:, c * P:(c + 1) * P], oT[:, b, c * P:(c + 1) * P], ident[:, :])
                last.then_inc(backP, 1)


_INS = ["x", "ctx_1024", "L0_xattn_Wq", "L0_xattn_Wk", "L0_xattn_Wv", "L0_xattn_gru_wih", "L0_xattn_gru_whh",
        "L0_xattn_gru_bih", "L0_xattn_gru_bhh", "L0_xattn_slot_norm_w", "L0_xattn_input_norm_w",
        "L0_ffn_Wg", "L0_ffn_W1", "L0_ffn_W2"]


def kernel(**inputs):
    import numpy as _np
    import concourse.bacc as _bacc
    from concourse import mybir as _mybir
    from concourse.bass_utils import run_bass_kernel_spmd as _run

    nc = _bacc.Bacc("TRN2", target_bir_lowering=False, num_devices=1)
    arrays, args = {}, []
    for name in _INS:
        a = _np.ascontiguousarray(inputs[name])
        arrays[f"in_{name}_dram"] = a
        args.append(nc.dram_tensor(f"in_{name}_dram", a.shape, _mybir.dt.from_np(a.dtype), kind="ExternalInput").ap())
    shape = tuple(inputs["x"].shape)
    args.append(nc.dram_tensor("out_0_dram", shape, _mybir.dt.float32, kind="ExternalOutput").ap())
    slot_attention_and_switch_ffn(nc, *args)
    r = _run(nc, [arrays], core_ids=[0])
    return r.results[0]["out_0_dram"]
```

```python
import concourse.bass as bass
from concourse import mybir
from contextlib import ExitStack


def slot_attention_and_switch_ffn(
    nc: bass.Bass,
    x: bass.AP,
    ctx_in: bass.AP,
    Wq: bass.AP,
    Wk: bass.AP,
    Wv: bass.AP,
    wih: bass.AP,
    whh: bass.AP,
    bih: bass.AP,
    bhh: bass.AP,
    slot_w: bass.AP,
    input_w: bass.AP,
    Wg: bass.AP,
    W1: bass.AP,
    W2: bass.AP,
    out: bass.AP,
):
    f32 = mybir.dt.float32
    f32r = mybir.dt.float32r
    bf16 = mybir.dt.bfloat16
    ALU = mybir.AluOpType
    ACT = mybir.ActivationFunctionType
    AX = mybir.AxisListType.X

    P = 128
    B, N, D = x.shape
    M = ctx_in.shape[1]
    G3 = wih.shape[0]
    E = Wg.shape[1]
    H = W1.shape[2]
    CAP = N // E
    NG = 2
    BG = B // NG
    C = N // P
    CG = BG * C
    J = H // P
    NP = E // 2
    KG = BG * M
    NH = N // 2
    HS = [(hf, i) for hf in range(2) for i in range(BG)]
    SQ = 32
    NB = NH // SQ
    ITERS = 3
    HALVES = ITERS * NG
    EPS_RMS = 1e-6
    EPS_ATT = 1e-6
    EPS_LN = 1e-5
    SCALE = float(D) ** -0.5
    DVE_HOT = [4, 4, 3, 3]
    DROPPED = 1024.0

    ctx = ExitStack()
    with ctx:
        def sb(name, shape, dt=f32):
            return ctx.enter_context(nc.sbuf_tensor(name, shape, dt))

        def sem(name):
            return ctx.enter_context(nc.semaphore(name))

        def sems(name, n):
            return [sem(f"{name}{i}") for i in range(n)]

        x_tok = sb("x_tok", [P, B * C, D])
        xn_tok = sb("xn_tok", [P, B * C, D])
        xT = sb("xT", [P, B, N])
        h = sb("h", [P, B, N])
        h2 = sb("h2", [P, B, N])
        Wq_t = sb("Wq_t", [P, D])
        bias_rows = sb("bias_rows", [6, D])
        norm_rows = sb("norm_rows", [2, D])
        bn_rows = sb("bn_rows", [2 * M, D])
        bn_half = sb("bn_half", [2 * M, D], f32r)
        one_r = sb("one_r", [2 * M, 1], f32r)
        cols = sb("cols", [P, 8])
        half_b = sb("half_b", [P, 2])
        Wg_t = sb("Wg_t", [P, E])
        Wg_c = sb("Wg_c", [P, E])
        WkvT = sb("WkvT", [P, 2, D])
        wihT = sb("wihT", [P, G3])
        whhT = sb("whhT", [P, G3])
        PnT = sb("PnT", [P, B * M])
        kT = sb("kT", [P, B * M])
        Msc = sb("Msc", [P, B * M])
        VW = [sb(f"VW{b}", [P, G3], f32r) for b in range(B)]
        W1_t = sb("W1_t", [P, E, H])
        W2_t = sb("W2_t", [P, E, J, D])

        ident = sb("ident", [P, P])
        ident_r = sb("ident_r", [P, P], f32r)
        center = sb("center", [P, P])
        mean_w = sb("mean_w", [P, M])
        block1 = sb("block1", [P, P])
        fold = sb("fold", [P, P])
        pick = sb("pick", [P, 2, 4, 4, M], f32r)
        tri = sb("tri", [P, P], bf16)
        ones_b = sb("ones_b", [P, P], bf16)
        slot_iota = sb("slot_iota", [P, N])
        pair_iota = sb("pair_iota", [P, NP])
        rev = sb("rev", [P, C, E])
        mhalf = sb("mhalf", [P, B * C])

        stats = sb("stats", [P, B * C, 6])
        mv = sb("mv", [P, B * C, 2])
        rstd = sb("rstd", [P, B * C])
        gelu_one = sb("gelu_one", [P, 1])
        nmr = sb("nmr", [P, B * C])
        ssq = sb("ssq", [P, 1])
        rho_c = sb("rho_c", [P, 1])

        mse = [sb(f"mse{g}", [P, NB]) for g in range(NG)]
        rho = [sb(f"rho{g}", [P, NB]) for g in range(NG)]
        rhoT = [sb(f"rhoT{g}", [P, NH]) for g in range(NG)]
        sc = [sb(f"sc{g}", [P, NH]) for g in range(NG)]
        smax = [sb(f"smax{g}", [P, 1]) for g in range(NG)]
        nmax = [sb(f"nmax{g}", [P, 1]) for g in range(NG)]
        omax = [sb(f"omax{g}", [KG, 1]) for g in range(NG)]
        esum = [sb(f"esum{g}", [P, 1]) for g in range(NG)]
        einv = [sb(f"einv{g}", [P, 1]) for g in range(NG)]
        ex = sc
        dlhs = [sb(f"dlhs{g}", [P, P]) for g in range(NG)]
        denc = [sb(f"denc{g}", [P, NB]) for g in range(NG)]
        deni = [sb(f"deni{g}", [P, NB]) for g in range(NG)]
        attn = [sb(f"attn{g}", [P, NH]) for g in range(NG)]
        at_hi = [sb(f"at_hi{g}", [P, NH], f32r) for g in range(NG)]
        at_lo = [sb(f"at_lo{g}", [P, NH], f32r) for g in range(NG)]
        msT = attn
        at4 = sb("at4", [P, B, N], f32r)

        r_b = sb("r_b", [P, B, N])
        z_b = sb("z_b", [P, B, N])
        q_b = sb("q_b", [P, B, N])
        n_b = sb("n_b", [P, B, N])
        d_b = sb("d_b", [P, B, N])

        wih_t = n_b[:, 0, 0:G3].rearrange("p (a d) -> p a d", d=D)
        whh_t = n_b[:, 1, 0:G3].rearrange("p (a d) -> p a d", d=D)
        Wk_t, Wv_t = n_b[:, 2, 0:D], n_b[:, 2, D:2 * D]
        ctx_t, ctx_n, ctx_sq = (n_b[:, 3, k * D:(k + 1) * D] for k in range(3))
        v4 = q_b[:, :, 0:P]

        lg = sb("lg", [P, B * C, E])
        lmax = sb("lmax", [P, B * C])
        lex = sb("lex", [P, B * C, E])
        lsum = sb("lsum", [P, B * C])
        gate = sb("gate", [P, B * C])
        first = sb("first", [P, B * C, E])
        fmax = sb("fmax", [P, B * C])
        mask = sb("mask", [P, B * C, E], bf16)
        mpos = sb("mpos", [P, B * C, E])
        posr = sb("posr", [P, B * C])
        over = sb("over", [P, B * C])
        slot0 = sb("slot0", [P, B * C])
        slot = sb("slot", [P, B * C])
        slot_r = sb("slot_r", [P, B * C], f32r)
        x_hi = sb("x_hi", [P, B * C, D], f32r)
        x_lo = sb("x_lo", [P, B * C, D], f32r)
        disp = sb("disp", [P, 2, C, N], f32r)
        comb = [at4, sb("comb", [P, B, N], f32r)]
        y_hi = sb("y_hi", [P, 2, B, D], f32r)
        y_lo = sb("y_lo", [P, 2, B, D], f32r)

        x2_tok = xn_tok
        xln = x_tok
        srow = q_b
        hid = [a[:, :, :].rearrange("p b n -> p (b n)").rearrange("p (e j s) -> p e j s", e=2, j=J)
               for a in (r_b, z_b)]
        xe = h2[:, :, :].rearrange("p b n -> p (b n)").rearrange("p (e b c) -> p e b c", e=E, b=B)
        oT = d_b
        res = h

        bank = [ctx.enter_context(nc.psum_tensor(f"bank{i}", [P, N], f32)) for i in range(8)]
        RB, ZB, HB, XB = ([bank[4 * g + k] for g in range(NG)] for k in range(4))
        tok_bank = [bank[0], bank[1], bank[4], bank[5]]
        route_bank = [bank[2], bank[3], bank[6], bank[7]]
        x_bank = [bank[4], bank[5], bank[6], bank[4]]
        vw_bank = [bank[1], bank[4], bank[5], bank[7]]
        hid_bank = [bank[2], bank[3]]
        y_bank = [bank[6], bank[7]]
        back_bank = [bank[2], bank[3], bank[6], bank[7]]

        x_in = sems("x_in", B)
        ctx_in_s, wkv_in, wq_in, wih_in, whh_in = (sem(n) for n in ("ctx_ld", "wkv_ld", "wq_ld", "wih_ld", "whh_ld"))
        norms_in, bias_in, bn_in, wg_in = sem("norms_ld"), sem("bias_ld"), sem("bn_ld"), sem("wg_ld")
        bn_set = sem("bn_set")
        w1_in, w2_in = sem("w1_ld"), sem("w2_ld")
        out_done = sem("out_done")
        pool_set, dve_set, fold_set, pick_set = (sem(n) for n in ("pool_set", "dve_set", "fold_set", "pick_set"))
        xstat, xmv, xrstd, xnorm, xnT, hinit, xTp, xTc = (
            sem(n) for n in ("xstat", "xmv", "xrstd", "xnorm", "xnT", "hinit", "xTp", "xTc"))
        cssq, crho, cnorm, wtr, wtr_c, kv_p, kv_c, m_p, m_c, vw_p, vw_h, vw_c, hb_set = (
            sem(n) for n in ("cssq", "crho", "cnorm", "wtr", "wtr_c", "kv_p", "kv_c", "m_p", "m_c", "vw_p", "vw_h", "vw_c", "hb_set"))
        names = ["h_ready", "sq", "ms", "msT", "mse", "rho", "rhoT", "smax", "nmax", "exp", "einv",
                 "dlhs", "den", "denT", "denc", "deni", "rdT", "attn", "omax", "fmx", "fold", "ahi", "alo",
                 "st", "at4", "rh", "xn", "zp", "tr", "hn", "q", "q2", "tz", "z", "zh", "n", "c"]
        S = [{k: sem(f"{k}_{'AB'[g]}") for k in names} for g in range(NG)]
        x2T, x2P, x2st, x2mv, x2rs, x2nm, x2ln, x2lv, x2c, xhi, xlo, xlv = (
            sem(n) for n in ("x2T", "x2P", "x2st", "x2mv", "x2rs", "x2nm", "x2ln", "x2lv", "x2c", "xhi", "xlo", "xlv"))
        lgP, lmx, dl, gl, lx, ls, gt, fi, fm, mk, posP, pl, dspP = (
            sem(n) for n in ("lgP", "lmx", "dl", "gl", "lx", "ls", "gt", "fi", "fm", "mk", "posP", "pl", "dspP"))
        dsp, xeP, xeC, srP, srC, cmb, hidP, hidC, yP, yh, yl, accP, oTs, backP, go, fin = (
            sem(n) for n in ("dsp", "xeP", "xeC", "srP", "srC", "cmb", "hidP", "hidC", "yP", "yh", "yl",
                             "accP", "oTs", "backP", "go", "fin"))

        block = ctx.enter_context(nc.Block())

        def batch(g, i):
            return BG * g + i

        @block.sync
        def _(sp):
            def load_x(b):
                sp.dma_start(x_tok[:, b * C:(b + 1) * C, :],
                             x[b].rearrange("(c p) d -> p c d", p=P)).then_inc(x_in[b], 16)

            load_x(0)
            load_x(1)
            sp.dma_start(Wq_t[:, :], Wq).then_inc(wq_in, 16)
            sp.dma_start(whh_t[:, :, :], whh.rearrange("(a p) d -> p a d", p=P)).then_inc(whh_in, 16)
            sp.dma_start(bias_rows[0:3, :], bih.rearrange("(a d) -> a d", d=D)).then_inc(bias_in, 16)
            sp.dma_start(bias_rows[3:6, :], bhh.rearrange("(a d) -> a d", d=D)).then_inc(bias_in, 16)
            sp.dma_start(Wg_t[:, :], Wg).then_inc(wg_in, 16)
            sp.dma_start(wih_t[:, :, :], wih.rearrange("(a p) d -> p a d", p=P)).then_inc(wih_in, 16)
            load_x(2)
            load_x(3)
            sp.wait_ge(bn_set, 1)
            for k in range(2):
                sp.dma_start(bn_rows[k * M:k * M + 1, :],
                             bhh[2 * D:G3].rearrange("(a d) -> a d", d=D)).then_inc(bn_in, 16)
            sp.wait_ge(wih_in, 16)
            sp.dma_start(W1_t[:, :, :], W1.rearrange("e d h -> d e h")).then_inc(w1_in, 16)
            sp.dma_start(W2_t[:, :, :, :], W2.rearrange("e (j p) d -> p e j d", p=P)).then_inc(w2_in, 16)
            for b in range(B):
                sp.wait_ge(fin, (C, 2 * C, 2 * C + 1, 2 * C + 2)[b])
                sp.dma_start(out[b].rearrange("(c p) d -> p c d", p=P),
                             res[:, b, :].rearrange("p (c d) -> p c d", d=D)).then_inc(out_done, 16)
            sp.wait_ge(out_done, 16 * B)

        @block.gpsimd
        def _(pool):
            nc.gpsimd.memset(ident[:, :], 0.0).then_inc(pool_set, 1)
            nc.gpsimd.memset(tri[:, :], 1.0).then_inc(pool_set, 1)
            pool.wait_ge(pool_set, 2)
            nc.gpsimd.affine_select(out=ident[:, :], in_=ident[:, :], compare_op=ALU.not_equal, fill=1.0,
                                    base=0, pattern=[[-1, P]], channel_multiplier=1).then_inc(pool_set, 1)
            nc.gpsimd.affine_select(out=tri[:, :], in_=tri[:, :], compare_op=ALU.is_gt, fill=0.0,
                                    base=0, pattern=[[1, P]], channel_multiplier=-1).then_inc(pool_set, 1)
            nc.gpsimd.iota(slot_iota[:, :], [[1, N]], base=0, channel_multiplier=0,
                           allow_small_or_imprecise_dtypes=True).then_inc(pool_set, 1)
            nc.gpsimd.iota(pair_iota[:, :], [[P, NP]], base=0, channel_multiplier=1,
                           allow_small_or_imprecise_dtypes=True).then_inc(pool_set, 1)
            nc.gpsimd.iota(rev[:, :, :], [[0, C], [-1, E]], base=E, channel_multiplier=0,
                           allow_small_or_imprecise_dtypes=True).then_inc(pool_set, 1)

            pool.wait_ge(dve_set, 5)
            pool.wait_ge(cssq, 1)
            nc.gpsimd.tensor_scalar(rho_c[:, :], ssq[:, :], 1.0 / D, EPS_RMS, ALU.mult, ALU.add).then_inc(crho, 1)
            pool.wait_ge(crho, 1)
            nc.gpsimd.tensor_tensor(rho_c[:, :], rho_c[:, :], mhalf[:, 0:1], ALU.pow).then_inc(crho, 1)
            def x_rstd(b):
                cs = slice(b * C, (b + 1) * C)
                pool.wait_ge(xmv, (b + 1) * C)
                nc.gpsimd.tensor_scalar(rstd[:, cs], mv[:, cs, 1], 1.0, EPS_LN, ALU.mult, ALU.add).then_inc(xrstd, 1)
                pool.wait_ge(xrstd, 2 * b + 1)
                nc.gpsimd.tensor_tensor(rstd[:, cs], rstd[:, cs], mhalf[:, 0:C], ALU.pow).then_inc(xrstd, 1)

            x_rstd(0)
            x_rstd(1)
            pool.wait_ge(pool_set, 4)
            for k in range(2):
                nc.gpsimd.tensor_copy(fold[:, k * KG:(k + 1) * KG], ident[:, 0:KG]).then_inc(fold_set, 1)
            pool.wait_ge(fold_set, 2)
            for k in range(2):
                nc.gpsimd.tensor_tensor(fold[:, k * KG:(k + 1) * KG], fold[:, k * KG:(k + 1) * KG],
                                        ident[:, KG:P], ALU.add).then_inc(fold_set, 1)
            nc.gpsimd.memset(pick[:, :, :, :, :].bitcast(f32), 0.0).then_inc(pick_set, 1)

            def rho_step(g, t):
                s = S[g]
                pool.wait_ge(s["msT"], t + 1)
                nc.gpsimd.tensor_scalar(mse[g][:, :], msT[g][:, :].rearrange("p (j q) -> p j q", q=SQ)[:, :, 0],
                                        1.0, EPS_RMS, ALU.mult, ALU.add).then_inc(s["mse"], 1)
                pool.wait_ge(s["mse"], t + 1)
                nc.gpsimd.tensor_tensor(rho[g][:, :], mse[g][:, :], mhalf[:, 0:NB], ALU.pow).then_inc(s["rho"], 1)

            def z_step(g, i, t):
                s, b, k = S[g], batch(g, i), BG * t + i + 1
                pool.wait_ge(s["tz"], k)
                nc.gpsimd.tensor_scalar(d_b[:, b, :], z_b[:, b, :], 0.5, 0.5, ALU.mult, ALU.add).then_inc(s["z"], 1)
                pool.wait_ge(s["z"], k)
                nc.gpsimd.tensor_tensor(d_b[:, b, :], d_b[:, b, :], h[:, b, :], ALU.mult).then_inc(s["zh"], 1)

            def x2_rstd(b):
                cs = slice(b * C, (b + 1) * C)
                pool.wait_ge(x2mv, (b + 1) * C)
                nc.gpsimd.tensor_scalar(rstd[:, cs], mv[:, cs, 1], 1.0, EPS_LN, ALU.mult, ALU.add).then_inc(x2rs, 1)
                pool.wait_ge(x2rs, 2 * b + 1)
                nc.gpsimd.tensor_tensor(rstd[:, cs], rstd[:, cs], mhalf[:, 0:C], ALU.pow).then_inc(x2rs, 1)

            def dispatch_hot(b):
                pool.wait_ge(pl, 6 * b + 5)
                if b >= 2:
                    pool.wait_ge(xeP, b - 1)
                for c in range(DVE_HOT[b], C):
                    nc.gpsimd.tensor_scalar(disp[:, b % 2, c, :], slot_iota[:, :], slot[:, b * C + c:b * C + c + 1],
                                            None, ALU.is_equal).then_inc(dspP, 1)

            def x_low(b):
                cs = slice(b * C, (b + 1) * C)
                pool.wait_ge(xhi, b + 1)
                nc.gpsimd.tensor_tensor(x_lo[:, cs, :], xln[:, cs, :], x_hi[:, cs, :].bitcast(f32),
                                        ALU.subtract).then_inc(xlo, 1)

            rho_step(0, 0)
            x_rstd(2)
            x_rstd(3)
            rho_step(1, 0)
            z_step(0, 0, 0)
            z_step(0, 1, 0)
            for half in range(1, HALVES - 1):
                t, g = divmod(half, NG)
                ot, og = divmod(half + 1, NG)
                rho_step(og, ot)
                z_step(g, 0, t)
                z_step(g, 1, t)
            t, g = ITERS - 1, NG - 1
            z_step(g, 0, t)
            x2_rstd(0)
            x2_rstd(1)
            x_low(0)
            z_step(g, 1, t)
            x_low(1)
            x2_rstd(2)
            x2_rstd(3)
            dispatch_hot(2)
            dispatch_hot(3)

        @block.scalar
        def _(act):
            act.dma_start(ctx_t[:, :], ctx_in.rearrange("b m d -> (b m) d")).then_inc(ctx_in_s, 16)
            act.dma_start(norm_rows[0:1, :], slot_w.rearrange("(a d) -> a d", d=D)).then_inc(norms_in, 16)
            act.dma_start(norm_rows[1:2, :], input_w.rearrange("(a d) -> a d", d=D)).then_inc(norms_in, 16)
            act.dma_start(Wk_t[:, :], Wk).then_inc(wkv_in, 16)
            act.dma_start(Wv_t[:, :], Wv).then_inc(wkv_in, 16)

            act.wait_ge(pool_set, 4)
            nc.scalar.activation(ident_r[:, :], ident[:, :], ACT.Copy)

            def x_out(b):
                act.wait_ge(xTp, b + 1)
                nc.scalar.activation(xT[:, b, :], x_bank[b][:, :], ACT.Copy).then_inc(xTc, 1)

            x_out(0)
            x_out(1)
            act.wait_ge(wtr, 3)
            nc.scalar.activation(WkvT[:, :, :], bank[0][:, 0:2 * P].rearrange("p (a d) -> p a d", d=D),
                                 ACT.Copy).then_inc(wtr_c, 1)

            act.wait_ge(kv_p, 1)
            nc.scalar.activation(kT[:, :], bank[0][:, 0:B * M], ACT.Copy).then_inc(kv_c, 1)

            def square(g, i, t):
                s, b = S[g], batch(g, i)
                act.wait_ge(s["h_ready"], BG * t + i + 1)
                nc.scalar.activation(h2[:, b, :], h[:, b, :], ACT.Square).then_inc(s["sq"], 1)

            def first_slots(b):
                act.wait_ge(xnT, b + 1)
                nc.scalar.activation(h[:, b, :], bank[4 + b][:, :], ACT.Copy).then_inc(S[b // BG]["h_ready"], 1)

            def vw_high(b):
                act.wait_ge(vw_p, b + 1)
                nc.scalar.activation(VW[b][:, :], vw_bank[b][:, 0:G3], ACT.Copy).then_inc(vw_h, 1)

            first_slots(0)
            square(0, 0, 0)
            first_slots(1)
            square(0, 1, 0)
            act.wait_ge(wtr, 4)
            nc.scalar.activation(whhT[:, 0:2 * D], bank[7][:, 0:2 * D], ACT.Copy)
            nc.scalar.activation(whhT[:, 2 * D:G3], bank[7][:, 2 * D:G3], ACT.Copy, scale=0.5).then_inc(wtr_c, 1)
            nc.scalar.activation(cols[:, 0:6], bank[7][:, G3:G3 + 6], ACT.Copy).then_inc(wtr_c, 1)
            def wih_out():
                act.wait_ge(wtr, 5)
                nc.scalar.activation(wihT[:, :], bank[1][:, 0:G3], ACT.Copy).then_inc(wtr_c, 1)

            def exps(g, t):
                s = S[g]
                act.wait_ge(s["nmax"], t + 1)
                nc.scalar.activation(ex[g][:, :], sc[g][:, :], ACT.Exp, bias=nmax[g][:, 0:1],
                                     accum_out=esum[g][:, 0:1]).then_inc(s["exp"], 1)

            def spread(g, i, t):
                s, k = S[g], BG * t + i + 1
                act.wait_ge(s["st"], k)
                nc.scalar.activation(at4[:, batch(g, i), :], XB[g][:, :], ACT.Copy).then_inc(s["at4"], 1)

            def reset(g, i, t):
                s, b, k = S[g], batch(g, i), BG * t + i + 1
                act.wait_ge(s["rh"], k)
                nc.scalar.activation(r_b[:, b, :], RB[g][:, :], ACT.Tanh, bias=half_b[:, 0:1],
                                     scale=0.5).then_inc(s["tr"], 1)

            def update(g, i, t):
                s, b, k = S[g], batch(g, i), BG * t + i + 1
                act.wait_ge(s["zp"], k)
                nc.scalar.activation(z_b[:, b, :], ZB[g][:, :], ACT.Tanh, bias=half_b[:, 1:2],
                                     scale=0.5).then_inc(s["tz"], 1)

            def candidate(g, i, t):
                s, b, k = S[g], batch(g, i), BG * t + i + 1
                act.wait_ge(s["q2"], k)
                nc.scalar.activation(n_b[:, b, :], q_b[:, b, :], ACT.Tanh, bias=cols[:, 2:3]).then_inc(s["n"], 1)

            def x2_out(b):
                cs = slice(b * C, (b + 1) * C)
                act.wait_ge(x2P, b + 1)
                nc.scalar.activation(x2_tok[:, cs, :], tok_bank[b][:, :].rearrange("p (c d) -> p c d", d=D),
                                     ACT.Copy).then_inc(x2c, 1)

            def x2_norm(b):
                act.wait_ge(x2nm, b + 1)
                for c in range(b * C, (b + 1) * C):
                    nc.scalar.activation(xln[:, c, :], x2_tok[:, c, :], ACT.Identity, bias=nmr[:, c:c + 1],
                                         scale=rstd[:, c:c + 1]).then_inc(x2ln, 1)

            def x_high(b):
                cs = slice(b * C, (b + 1) * C)
                if b < 2:
                    act.wait_ge(x2ln, (b + 1) * C)
                else:
                    act.wait_ge(x2lv, (b - 1) * C)
                nc.scalar.activation(x_hi[:, cs, :], xln[:, cs, :], ACT.Copy).then_inc(xhi, 1)

            def gate_exp():
                act.wait_ge(gl, 1)
                nc.scalar.activation(lex[:, :, :], lg[:, :, :], ACT.Exp).then_inc(lx, 1)

            def dispatched_out(b):
                act.wait_ge(xeP, b + 1)
                nc.scalar.activation(xe[:, :, b, :], tok_bank[b][:, :].rearrange("p (e c) -> p e c", c=CAP),
                                     ACT.Copy).then_inc(xeC, 1)

            def rows_out(b):
                act.wait_ge(srP, b + 1)
                nc.scalar.activation(srow[:, b, :], route_bank[b][:, :], ACT.Copy).then_inc(srC, 1)

            def gelu_table():
                act.wait_ge(dve_set, 5)
                nc.scalar.activation(gelu_one[:, :], mhalf[:, 0:1], ACT.Gelu_apprx_tanh)

            wih_out()
            exps(0, 0)
            vw_high(0)
            vw_high(1)
            first_slots(2)
            square(1, 0, 0)
            first_slots(3)
            square(1, 1, 0)
            vw_high(2)
            spread(0, 0, 0)
            x_out(2)
            act.wait_ge(hb_set, 2)
            reset(0, 0, 0)
            x_out(3)
            spread(0, 1, 0)
            act.wait_ge(hb_set, 2)
            update(0, 0, 0)
            vw_high(3)
            candidate(0, 0, 0)
            reset(0, 1, 0)
            exps(1, 0)
            update(0, 1, 0)
            square(0, 0, 1)
            candidate(0, 1, 0)
            spread(1, 0, 0)
            square(0, 1, 1)
            for half in range(1, HALVES - 1):
                t, g = divmod(half, NG)
                ot, og = divmod(half + 1, NG)
                reset(g, 0, t)
                spread(g, 1, t)
                update(g, 0, t)
                candidate(g, 0, t)
                reset(g, 1, t)
                exps(og, ot)
                if t + 1 < ITERS:
                    square(g, 0, t + 1)
                update(g, 1, t)
                candidate(g, 1, t)
                spread(og, 0, ot)
                if t + 1 < ITERS:
                    square(g, 1, t + 1)
            t, g = ITERS - 1, NG - 1
            reset(g, 0, t)
            update(g, 0, t)
            x2_out(0)
            spread(g, 1, t)
            x2_out(1)
            candidate(g, 0, t)
            reset(g, 1, t)
            x2_norm(0)
            update(g, 1, t)
            x_high(0)
            x2_norm(1)
            candidate(g, 1, t)
            rows_out(0)
            x2_out(2)
            rows_out(1)
            x_high(1)
            x2_out(3)
            x_high(2)
            x_high(3)
            dispatched_out(0)
            dispatched_out(1)
            rows_out(2)
            gate_exp()
            dispatched_out(2)
            gelu_table()
            dispatched_out(3)
            rows_out(3)

            def gelu(k):
                for e in range(2):
                    for half in range(2):
                        n = (2 * k + e) * 2 + half
                        act.wait_ge(hidP, n + 1)
                        dst = hid[k % 2][:, e, 2 * half:2 * half + 2, :]
                        if k >= 2:
                            act.wait_ge(yP, k - 1)
                        nc.scalar.activation(dst, hid_bank[half][:, :].rearrange("p (a s) -> p a s", s=B * CAP),
                                             ACT.Gelu_apprx_tanh).then_inc(hidC, 1)

            def y_high(k):
                act.wait_ge(yP, k + 1)
                if k >= 2:
                    act.wait_ge(accP, k - 1)
                nc.scalar.activation(y_hi[:, k % 2, :, :], y_bank[k % 2][:, :].rearrange("p (b d) -> p b d", d=D),
                                     ACT.Copy).then_inc(yh, 1)

            gelu(0)
            for k in range(NP):
                if k + 1 < NP:
                    gelu(k + 1)
                y_high(k)
            for b in range(B):
                act.wait_ge(accP, NP - 1 + b + 1)
                nc.scalar.activation(oT[:, b, :], tok_bank[b][:, :], ACT.Copy).then_inc(oTs, 1)
            act.wait_ge(gt, 1)
            for b in range(2, B):
                act.wait_ge(backP, b + 1)
                for c in range(C):
                    n = b * C + c
                    nc.scalar.activation(oT[:, b, c * P:(c + 1) * P], back_bank[b][:, c * P:(c + 1) * P], ACT.Copy,
                                         scale=gate[:, n:n + 1]).then_inc(go, 1)

        @block.vector
        def _(dve):
            v = nc.vector
            v.memset(mean_w[:, :], 1.0 / D).then_inc(dve_set, 1)
            v.memset(ones_b[:, :], 1.0).then_inc(dve_set, 1)
            v.memset(block1[:, :], 0.0).then_inc(dve_set, 1)
            dve.wait_ge(dve_set, 3)
            for i in range(P // M):
                last = v.memset(block1[i * M:(i + 1) * M, i * M:(i + 1) * M], 1.0)
            last.then_inc(dve_set, 1)
            v.memset(mhalf[:, :], -0.5).then_inc(dve_set, 1)
            v.memset(bn_rows[:, :], 0.0).then_inc(bn_set, 1)
            v.memset(one_r[:, :].bitcast(f32), 1.0).then_inc(bn_set, 1)
            dve.wait_ge(pool_set, 4)
            v.tensor_scalar(center[:, :], ident[:, :], -1.0 / D, None, ALU.add).then_inc(dve_set, 1)

            dve.wait_ge(ctx_in_s, 16)
            v.tensor_tensor_reduce(out=ctx_sq[:, :], in0=ctx_t[:, :], in1=ctx_t[:, :], scale=1.0, scalar=0.0,
                                   op0=ALU.mult, op1=ALU.add, accum_out=ssq[:, 0:1]).then_inc(cssq, 1)

            def x_stats(b):
                dve.wait_ge(x_in[b], 16)
                for c in range(b * C, (b + 1) * C):
                    v.bn_stats(stats[:, c, :], x_tok[:, c, :]).then_inc(xstat, 1)
                for c in range(b * C, (b + 1) * C):
                    dve.wait_ge(xstat, c + 1)
                    v.bn_aggr(mv[:, c, :], stats[:, c, :]).then_inc(xmv, 1)

            def x_norm(b):
                dve.wait_ge(xrstd, 2 * b + 2)
                for c in range(b * C, (b + 1) * C):
                    v.tensor_scalar(xn_tok[:, c, :], x_tok[:, c, :], mv[:, c, 0:1], rstd[:, c:c + 1],
                                    ALU.subtract, ALU.mult).then_inc(xnorm, 1)

            def vw_low(b):
                dve.wait_ge(vw_h, b + 1)
                v.tensor_tensor(VW[b][2 * M:P, :], vw_bank[b][2 * M:P, 0:G3], VW[b][2 * M:P, :].bitcast(f32),
                                ALU.subtract).then_inc(vw_c, 1)

            x_stats(0)
            dve.wait_ge(crho, 2)
            v.tensor_scalar(ctx_n[:, :], ctx_t[:, :], rho_c[:, 0:1], None, ALU.mult).then_inc(cnorm, 1)
            dve.wait_ge(wtr, 1)
            v.tensor_copy(cols[:, 6:8], bank[3][:, 0:2]).then_inc(m_c, 1)
            x_stats(1)
            dve.wait_ge(m_c, 1)
            dve.wait_ge(wtr, 2)
            v.tensor_scalar(PnT[:, :], bank[3][:, 0:P], cols[:, 7:8], None, ALU.mult).then_inc(m_c, 1)
            x_norm(0)
            x_norm(1)
            dve.wait_ge(kv_c, 1)
            v.tensor_copy(v4[:, :, :].rearrange("p b (s m) -> p b s m", m=M),
                          bank[0][:, B * M:2 * B * M].rearrange("p (b m) -> p b m", m=M).unsqueeze(2)
                          .broadcast_to([P, B, P // M, M])).then_inc(kv_c, 1)
            dve.wait_ge(m_p, 1)
            v.tensor_scalar(Msc[:, :], bank[3][:, 0:B * M], cols[:, 6:7], SCALE, ALU.mult, ALU.mult).then_inc(m_c, 1)
            v.tensor_copy(Wg_c[:, :], bank[3][:, 256:256 + E]).then_inc(m_c, 1)
            dve.wait_ge(pick_set, 1)
            for part in range(2):
                for rep in range(2):
                    v.tensor_copy(pick[:, part, :, 2 * rep + part, :],
                                  ident[:, :].rearrange("p (a m) -> p a m", m=M)).then_inc(pick_set, 1)

            def squares(g, t):
                dve.wait_ge(S[g]["ms"], t + 1)
                v.transpose(msT[g][:, :], HB[g][:, 0:NH]).then_inc(S[g]["msT"], 1)

            def spread_rho(g, t):
                s = S[g]
                dve.wait_ge(s["rho"], t + 1)
                v.transpose(rhoT[g][:, :].rearrange("p (j q) -> p j q", q=SQ),
                            rho[g][:, :].unsqueeze(2).broadcast_to([P, NB, SQ])).then_inc(s["rhoT"], 1)

            def scaled_scores(g, t):
                s = S[g]
                dve.wait_ge(s["rhoT"], t + 1)
                v.tensor_tensor_reduce(out=sc[g][:, :], in0=RB[g][:, 0:NH], in1=rhoT[g][:, :], scale=1.0,
                                       scalar=-3.0e38, op0=ALU.mult, op1=ALU.max,
                                       accum_out=smax[g][:, 0:1]).then_inc(s["smax"], 1)

            def maxima(g, t):
                s = S[g]
                dve.wait_ge(s["smax"], t + 1)
                v.tensor_scalar(omax[g][:, :], smax[g][KG:P, :], -1.0, None, ALU.mult).then_inc(s["omax"], 1)
                dve.wait_ge(s["omax"], t + 1)
                v.scalar_tensor_tensor(out=nmax[g][0:KG, :], in0=smax[g][0:KG, :], scalar=-1.0, in1=omax[g][:, :],
                                       op0=ALU.mult, op1=ALU.min).then_inc(s["fmx"], 1)
                dve.wait_ge(s["fmx"], t + 1)
                v.tensor_copy(nmax[g][KG:P, :], nmax[g][0:KG, :]).then_inc(s["nmax"], 1)

            def softmax_scale(g, t):
                s = S[g]
                dve.wait_ge(s["fold"], t + 1)
                v.reciprocal(einv[g][:, :], XB[g][:, 0:1]).then_inc(s["einv"], 1)
                dve.wait_ge(s["einv"], t + 1)
                v.tensor_scalar(dlhs[g][:, :], block1[:, :], einv[g][:, 0:1], None, ALU.mult).then_inc(s["dlhs"], 1)

            def inv_denominators(g, t):
                s = S[g]
                dve.wait_ge(s["den"], t + 1)
                v.transpose(msT[g][:, :], XB[g][:, 0:NH]).then_inc(s["denT"], 1)
                dve.wait_ge(s["denT"], t + 1)
                v.tensor_scalar(denc[g][:, :], msT[g][:, :].rearrange("p (j q) -> p j q", q=SQ)[:, :, 0],
                                EPS_ATT, None, ALU.add).then_inc(s["denc"], 1)
                dve.wait_ge(s["denc"], t + 1)
                v.reciprocal(deni[g][:, :], denc[g][:, :]).then_inc(s["deni"], 1)

            def spread_inv(g, t):
                s = S[g]
                dve.wait_ge(s["deni"], t + 1)
                v.transpose(rhoT[g][:, :].rearrange("p (j q) -> p j q", q=SQ),
                            deni[g][:, :].unsqueeze(2).broadcast_to([P, NB, SQ])).then_inc(s["rdT"], 1)

            def attention(g, t):
                s = S[g]
                dve.wait_ge(s["rdT"], t + 1)
                v.scalar_tensor_tensor(out=attn[g][:, :], in0=ex[g][:, :], scalar=einv[g][:, 0:1],
                                       in1=rhoT[g][:, :], op0=ALU.mult, op1=ALU.mult).then_inc(s["attn"], 1)

            def high(g, t):
                s = S[g]
                dve.wait_ge(s["attn"], t + 1)
                v.tensor_copy(at_hi[g][:, :], attn[g][:, :]).then_inc(s["ahi"], 1)

            def low(g, t):
                s = S[g]
                dve.wait_ge(s["ahi"], t + 1)
                v.tensor_tensor(at_lo[g][:, :], attn[g][:, :], at_hi[g][:, :].bitcast(f32),
                                ALU.subtract).then_inc(s["alo"], 1)

            def reset_hn(g, i, t):
                s, b, k = S[g], batch(g, i), BG * t + i + 1
                dve.wait_ge(s["tr"], k)
                dve.wait_ge(s["hn"], k)
                v.scalar_tensor_tensor(out=q_b[:, b, :], in0=r_b[:, b, :], scalar=1.0, in1=HB[g][:, :],
                                       op0=ALU.add, op1=ALU.mult).then_inc(s["q"], 1)

            def add_xn(g, i, t):
                s, b, k = S[g], batch(g, i), BG * t + i + 1
                dve.wait_ge(s["q"], k)
                dve.wait_ge(s["xn"], k)
                v.tensor_tensor(q_b[:, b, :], q_b[:, b, :], XB[g][:, :], ALU.add).then_inc(s["q2"], 1)

            def weigh_n(g, i, t):
                s, b, k = S[g], batch(g, i), BG * t + i + 1
                dve.wait_ge(s["tz"], k)
                dve.wait_ge(s["n"], k)
                v.scalar_tensor_tensor(out=n_b[:, b, :], in0=z_b[:, b, :], scalar=-1.0, in1=n_b[:, b, :],
                                       op0=ALU.add, op1=ALU.mult).then_inc(s["c"], 1)

            def new_slots(g, i, t):
                s, b, k = S[g], batch(g, i), BG * t + i + 1
                dve.wait_ge(s["c"], k)
                dve.wait_ge(s["zh"], k)
                v.scalar_tensor_tensor(out=h[:, b, :], in0=n_b[:, b, :], scalar=-0.5, in1=d_b[:, b, :],
                                       op0=ALU.mult, op1=ALU.add).then_inc(s["h_ready"], 1)

            def final_x(b):
                g, i = b // BG, b % BG
                dve.wait_ge(xTc, b + 1)
                dve.wait_ge(S[g]["h_ready"], BG * ITERS + i + 1)
                v.tensor_tensor(xT[:, b, :], xT[:, b, :], h[:, b, :], ALU.add).then_inc(x2T, 1)

            def half_biases():
                dve.wait_ge(wtr_c, 3)
                v.tensor_tensor(half_b[:, :], cols[:, 0:2], cols[:, 3:5], ALU.add).then_inc(hb_set, 1)
                dve.wait_ge(hb_set, 1)
                v.tensor_scalar(half_b[:, :], half_b[:, :], 0.5, None, ALU.mult).then_inc(hb_set, 1)

            def half_bn():
                dve.wait_ge(bn_in, 32)
                v.tensor_scalar(bn_half[:, :], bn_rows[:, :], 0.5, None, ALU.mult).then_inc(bn_set, 1)
                dve.wait_ge(bn_set, 3)
                v.scalar_tensor_tensor(out=bn_half[M:2 * M, :], in0=bn_rows[M:2 * M, :], scalar=0.5,
                                       in1=bn_half[M:2 * M, :].bitcast(f32), op0=ALU.mult,
                                       op1=ALU.subtract).then_inc(bn_set, 1)

            def x2_stats(b):
                dve.wait_ge(x2c, b + 1)
                for c in range(b * C, (b + 1) * C):
                    v.bn_stats(stats[:, c, :], x2_tok[:, c, :]).then_inc(x2st, 1)
                for c in range(b * C, (b + 1) * C):
                    dve.wait_ge(x2st, c + 1)
                    v.bn_aggr(mv[:, c, :], stats[:, c, :]).then_inc(x2mv, 1)

            def x2_shift(b):
                cs = slice(b * C, (b + 1) * C)
                dve.wait_ge(x2rs, 2 * b + 2)
                v.scalar_tensor_tensor(out=nmr[:, cs], in0=mv[:, cs, 0], scalar=-1.0, in1=rstd[:, cs],
                                       op0=ALU.mult, op1=ALU.mult).then_inc(x2nm, 1)

            def x2_norm(b):
                dve.wait_ge(x2rs, 2 * b + 2)
                for c in range(b * C, (b + 1) * C):
                    v.tensor_scalar(xln[:, c, :], x2_tok[:, c, :], mv[:, c, 0:1], rstd[:, c:c + 1],
                                    ALU.subtract, ALU.mult).then_inc(x2lv, 1)

            def x_low(b):
                cs = slice(b * C, (b + 1) * C)
                dve.wait_ge(xhi, b + 1)
                v.tensor_tensor(x_lo[:, cs, :], xln[:, cs, :], x_hi[:, cs, :].bitcast(f32),
                                ALU.subtract).then_inc(xlv, 1)

            def wide(a, cs):
                return a[:, cs].unsqueeze(2).broadcast_to([P, cs.stop - cs.start, E])

            def choose(b):
                cs = slice(b * C, (b + 1) * C)
                logits = route_bank[b][:, 0:C * E].rearrange("p (c e) -> p c e", e=E)
                dve.wait_ge(lgP, b + 1)
                v.reduce_max(lmax[:, cs], logits, AX).then_inc(lmx, 1)
                dve.wait_ge(lmx, b + 1)
                v.tensor_tensor(lg[:, cs, :], logits, wide(lmax, cs), ALU.subtract).then_inc(dl, 1)
                dve.wait_ge(dl, b + 1)
                v.scalar_tensor_tensor(out=first[:, cs, :], in0=lg[:, cs, :], scalar=0.0, in1=rev[:, :, :],
                                       op0=ALU.is_ge, op1=ALU.mult).then_inc(fi, 1)
                dve.wait_ge(fi, b + 1)
                v.reduce_max(fmax[:, cs], first[:, cs, :], AX).then_inc(fm, 1)
                dve.wait_ge(fm, b + 1)
                v.tensor_tensor(mask[:, cs, :], first[:, cs, :], wide(fmax, cs), ALU.is_equal).then_inc(mk, 1)

            def place(b):
                cs = slice(b * C, (b + 1) * C)
                dve.wait_ge(posP, b + 1)
                v.tensor_tensor(mpos[:, cs, :], route_bank[b][:, 0:C * E].rearrange("p (c e) -> p c e", e=E),
                                mask[:, cs, :], ALU.mult).then_inc(pl, 1)
                dve.wait_ge(pl, 6 * b + 1)
                v.reduce_sum(posr[:, cs], mpos[:, cs, :], AX).then_inc(pl, 1)
                dve.wait_ge(pl, 6 * b + 2)
                v.tensor_scalar(over[:, cs], posr[:, cs], float(CAP), DROPPED, ALU.is_ge, ALU.mult).then_inc(pl, 1)
                v.scalar_tensor_tensor(out=slot0[:, cs], in0=fmax[:, cs], scalar=-float(CAP), in1=posr[:, cs],
                                       op0=ALU.mult, op1=ALU.add).then_inc(pl, 1)
                dve.wait_ge(pl, 6 * b + 4)
                v.scalar_tensor_tensor(out=slot[:, cs], in0=slot0[:, cs], scalar=float(CAP * E), in1=over[:, cs],
                                       op0=ALU.add, op1=ALU.add).then_inc(pl, 1)
                dve.wait_ge(pl, 6 * b + 5)
                v.tensor_copy(slot_r[:, cs], slot[:, cs]).then_inc(pl, 1)

            def dispatch_hot(b):
                if b >= 2:
                    dve.wait_ge(xeP, b - 1)
                for c in range(DVE_HOT[b]):
                    v.tensor_scalar(disp[:, b % 2, c, :], slot_iota[:, :], slot[:, b * C + c:b * C + c + 1], None,
                                    ALU.is_equal).then_inc(dsp, 1)

            def scale_logits():
                dve.wait_ge(x2rs, 2 * B)
                v.tensor_tensor(lg[:, :, :], lg[:, :, :], wide(rstd, slice(0, B * C)), ALU.mult).then_inc(gl, 1)

            def gates():
                dve.wait_ge(lx, 1)
                v.reduce_sum(lsum[:, :], lex[:, :, :], AX).then_inc(ls, 1)
                dve.wait_ge(ls, 1)
                v.reciprocal(gate[:, :], lsum[:, :]).then_inc(gt, 1)

            half_biases()
            half_bn()
            squares(0, 0)
            x_stats(2)
            x_stats(3)
            spread_rho(0, 0)
            scaled_scores(0, 0)
            maxima(0, 0)
            x_norm(2)
            softmax_scale(0, 0)
            x_norm(3)
            vw_low(0)
            vw_low(1)
            inv_denominators(0, 0)
            spread_inv(0, 0)
            attention(0, 0)
            high(0, 0)
            low(0, 0)
            vw_low(2)
            squares(1, 0)
            reset_hn(0, 0, 0)
            add_xn(0, 0, 0)
            vw_low(3)
            spread_rho(1, 0)
            scaled_scores(1, 0)
            maxima(1, 0)
            weigh_n(0, 0, 0)
            new_slots(0, 0, 0)
            softmax_scale(1, 0)
            reset_hn(0, 1, 0)
            inv_denominators(1, 0)
            spread_inv(1, 0)
            add_xn(0, 1, 0)
            attention(1, 0)
            high(1, 0)
            low(1, 0)
            weigh_n(0, 1, 0)
            new_slots(0, 1, 0)
            for half in range(1, HALVES - 1):
                t, g = divmod(half, NG)
                ot, og = divmod(half + 1, NG)
                squares(og, ot)
                reset_hn(g, 0, t)
                add_xn(g, 0, t)
                spread_rho(og, ot)
                scaled_scores(og, ot)
                maxima(og, ot)
                weigh_n(g, 0, t)
                new_slots(g, 0, t)
                softmax_scale(og, ot)
                reset_hn(g, 1, t)
                add_xn(g, 1, t)
                inv_denominators(og, ot)
                spread_inv(og, ot)
                attention(og, ot)
                high(og, ot)
                low(og, ot)
                weigh_n(g, 1, t)
                new_slots(g, 1, t)
            t, g = ITERS - 1, NG - 1
            final_x(0)
            reset_hn(g, 0, t)
            final_x(1)
            x2_stats(0)
            add_xn(g, 0, t)
            choose(0)
            x2_shift(0)
            x2_stats(1)
            weigh_n(g, 0, t)
            new_slots(g, 0, t)
            choose(1)
            final_x(2)
            reset_hn(g, 1, t)
            add_xn(g, 1, t)
            place(0)
            x2_shift(1)
            place(1)
            dispatch_hot(0)
            weigh_n(g, 1, t)
            new_slots(g, 1, t)
            dispatch_hot(1)
            final_x(3)
            x2_stats(2)
            choose(2)
            x2_stats(3)
            x2_norm(2)
            place(2)
            choose(3)
            dispatch_hot(2)
            x_low(2)
            x2_norm(3)
            scale_logits()
            place(3)
            dispatch_hot(3)
            x_low(3)
            gates()

            def combine_hot(k):
                if k >= 2:
                    dve.wait_ge(accP, k - 1)
                for b in range(B):
                    dve.wait_ge(srC, b + 1)
                    v.tensor_scalar(comb[k % 2][:, b, :], srow[:, b, :], pair_iota[:, k:k + 1], None,
                                    ALU.is_equal).then_inc(cmb, 1)

            def y_low(k):
                dve.wait_ge(yh, k + 1)
                if k >= 2:
                    dve.wait_ge(accP, k - 1)
                v.tensor_tensor(y_lo[:, k % 2, :, :], y_bank[k % 2][:, :].rearrange("p (b d) -> p b d", d=D),
                                y_hi[:, k % 2, :, :].bitcast(f32), ALU.subtract).then_inc(yl, 1)

            for k in range(NP):
                combine_hot(k)
                y_low(k)
            dve.wait_ge(gt, 1)
            for b in range(2):
                dve.wait_ge(backP, b + 1)
                for c in range(C):
                    n = b * C + c
                    v.scalar_tensor_tensor(out=res[:, b, c * D:(c + 1) * D], in0=back_bank[b][:, c * D:(c + 1) * D],
                                           scalar=gate[:, n:n + 1], in1=x2_tok[:, n, :],
                                           op0=ALU.mult, op1=ALU.add).then_inc(fin, 1)
            for b in range(2, B):
                dve.wait_ge(go, (b - 1) * C)
                v.tensor_tensor(res[:, b, :], oT[:, b, :],
                                x2_tok[:, b * C:(b + 1) * C, :].rearrange("p c d -> p (c d)"), ALU.add).then_inc(fin, 1)

        @block.tensor
        def _(pe):
            mm = nc.tensor.matmul
            tr = nc.tensor.transpose

            pe.wait_ge(pool_set, 4)

            def x_T(b):
                pe.wait_ge(x_in[b], 16)
                if b == 2:
                    pe.wait_ge(S[1]["h_ready"], 1)
                if b == 3:
                    pe.wait_ge(vw_c, 2)
                for c in range(C):
                    last = tr(x_bank[b][:, c * P:(c + 1) * P], x_tok[:, b * C + c, :], ident[:, :])
                last.then_inc(xTp, 1)

            def norm_T(b):
                if b < 2:
                    pe.wait_ge(xTc, b + 1)
                if b == 3:
                    pe.wait_ge(wtr_c, 3)
                pe.wait_ge(xnorm, (b + 1) * C)
                for c in range(C):
                    last = tr(bank[4 + b][:, c * P:(c + 1) * P], xn_tok[:, b * C + c, :], ident[:, :])
                last.then_inc(xnT, 1)

            x_T(0)
            pe.wait_ge(norms_in, 32)
            tr(bank[3][:, 0:2], norm_rows[:, :], ident[0:2, 0:2]).then_inc(wtr, 1)
            x_T(1)
            pe.wait_ge(m_c, 1)
            pe.wait_ge(cnorm, 1)
            tr(bank[3][:, 0:P], ctx_n[:, :], ident[:, :]).then_inc(wtr, 1)
            pe.wait_ge(wkv_in, 32)
            tr(bank[0][:, 0:P], Wk_t[:, :], ident[:, :])
            tr(bank[0][:, P:2 * P], Wv_t[:, :], ident[:, :]).then_inc(wtr, 1)
            pe.wait_ge(m_c, 2)
            pe.wait_ge(wtr_c, 1)
            mm(bank[0][:, 0:B * M], WkvT[:, 0, :], PnT[:, :], start=True, stop=True)
            mm(bank[0][:, B * M:2 * B * M], WkvT[:, 1, :], PnT[:, :], start=True, stop=True).then_inc(kv_p, 1)
            norm_T(0)
            pe.wait_ge(wq_in, 16)
            pe.wait_ge(wg_in, 16)
            pe.wait_ge(dve_set, 6)
            pe.wait_ge(kv_c, 1)
            mm(bank[3][:, 0:B * M], Wq_t[:, :], kT[:, :], start=True, stop=True)
            mm(bank[3][:, 256:256 + E], center[:, :], Wg_t[:, :], start=True, stop=True).then_inc(m_p, 1)
            norm_T(1)
            pe.wait_ge(whh_in, 16)
            pe.wait_ge(bias_in, 32)
            for a in range(3):
                tr(bank[7][:, a * P:(a + 1) * P], whh_t[:, a, :], ident[:, :])
            tr(bank[7][:, G3:G3 + 6], bias_rows[:, :], ident[0:6, 0:6]).then_inc(wtr, 1)
            def v_wih(b):
                if b == 0:
                    pe.wait_ge(kv_c, 2)
                    pe.wait_ge(wtr_c, 4)
                if b == 1:
                    pe.wait_ge(S[0]["h_ready"], 1)
                if b == 2:
                    pe.wait_ge(S[0]["h_ready"], 2)
                if b == 3:
                    pe.wait_ge(S[1]["h_ready"], 2)
                mm(vw_bank[b][:, 0:G3], v4[:, b, :], wihT[:, :], start=True, stop=True).then_inc(vw_p, 1)

            def scores(g, t):
                s = S[g]
                pe.wait_ge(s["h_ready"], BG * (t + 1))
                for hf, i in HS:
                    b, p = batch(g, i), hf * KG + i * M
                    mm(RB[g][p:p + M, 0:NH], Msc[:, b * M:(b + 1) * M], h[:, b, hf * NH:(hf + 1) * NH],
                       start=True, stop=True)

            def mean_squares(g, t):
                s = S[g]
                pe.wait_ge(s["sq"], BG * (t + 1))
                for hf, i in HS:
                    b, p = batch(g, i), hf * KG + i * M
                    last = mm(HB[g][p:p + M, 0:NH], mean_w[:, :], h2[:, b, hf * NH:(hf + 1) * NH],
                              start=True, stop=True)
                last.then_inc(s["ms"], 1)

            def exp_sums(g, t):
                s = S[g]
                pe.wait_ge(s["exp"], t + 1)
                mm(XB[g][:, 0:1], fold[:, :], esum[g][:, 0:1], start=True, stop=True).then_inc(s["fold"], 1)

            def denominators(g, t):
                s = S[g]
                pe.wait_ge(s["dlhs"], t + 1)
                mm(XB[g][:, 0:NH], dlhs[g][:, :], ex[g][:, :], start=True, stop=True).then_inc(s["den"], 1)

            def four_sets(g, i, t):
                s = S[g]
                if i == 0:
                    pe.wait_ge(s["alo"], t + 1)
                else:
                    pe.wait_ge(s["at4"], BG * t + i)
                for hf in range(2):
                    for part, a in enumerate((at_hi[g], at_lo[g])):
                        last = mm(XB[g][:, hf * NH:(hf + 1) * NH],
                                  pick[:, part, hf * BG + i, :, :].rearrange("p s m -> p (s m)"), a[:, :],
                                  start=(part == 0), stop=(part == 1))
                last.then_inc(s["st"], 1)

            def slots_r(g, i, t):
                s, b = S[g], batch(g, i)
                if i == 0:
                    pe.wait_ge(s["smax"], t + 1)
                else:
                    pe.wait_ge(s["tr"], BG * t + i)
                mm(RB[g][:, :], whhT[:, 0:P], h[:, b, :], start=True, stop=False)

            def slots_n(g, i, t):
                s, b = S[g], batch(g, i)
                if i == 0:
                    pe.wait_ge(s["msT"], t + 1)
                else:
                    pe.wait_ge(s["q"], BG * t + i)
                mm(HB[g][:, :], bn_half[:, :], one_r[:, :].broadcast_to([2 * M, N]), start=True, stop=False)
                mm(HB[g][:, :], whhT[:, 2 * P:3 * P], h[:, b, :], start=False, stop=True).then_inc(s["hn"], 1)

            def slots_z(g, i, t):
                s, b = S[g], batch(g, i)
                if i == 0:
                    pe.wait_ge(s["h_ready"], BG * (t + 1))
                else:
                    pe.wait_ge(s["tz"], BG * t + i)
                mm(ZB[g][:, :], whhT[:, P:2 * P], h[:, b, :], start=True, stop=False)

            def attn_r(g, i, t):
                s, b = S[g], batch(g, i)
                pe.wait_ge(s["at4"], BG * t + i + 1)
                mm(RB[g][:, :], VW[b][:, 0:P], at4[:, b, :], start=False, stop=True).then_inc(s["rh"], 1)

            def attn_z(g, i, t):
                s, b = S[g], batch(g, i)
                pe.wait_ge(s["at4"], BG * t + i + 1)
                mm(ZB[g][:, :], VW[b][:, P:2 * P], at4[:, b, :], start=False, stop=True).then_inc(s["zp"], 1)

            def attn_n(g, i, t):
                s, b = S[g], batch(g, i)
                pe.wait_ge(s["at4"], BG * (t + 1))
                if i > 0:
                    pe.wait_ge(s["q2"], BG * t + i)
                mm(XB[g][:, :], VW[b][:, 2 * P:3 * P], at4[:, b, :], start=True, stop=True).then_inc(s["xn"], 1)

            def x2_back(b):
                s, i = S[b // BG], b % BG
                pe.wait_ge(s[("tr", "tz")[i]], BG * ITERS)
                pe.wait_ge(x2T, b + 1)
                for c in range(C):
                    last = tr(tok_bank[b][:, c * P:(c + 1) * P], xT[:, b, c * P:(c + 1) * P], ident[:, :])
                last.then_inc(x2P, 1)

            def logits(b):
                s, i = S[b // BG], b % BG
                pe.wait_ge(s[("q", "q2")[i]], BG * ITERS)
                pe.wait_ge(x2T, b + 1)
                for c in range(C):
                    last = mm(route_bank[b][:, c * E:(c + 1) * E], xT[:, b, c * P:(c + 1) * P], Wg_c[:, :],
                              start=True, stop=True)
                last.then_inc(lgP, 1)

            def positions(b):
                pe.wait_ge(mk, b + 1)
                for k in range(1, C):
                    mm(route_bank[b][:, k * E:C * E], ones_b[:, :],
                       mask[:, b * C:(b + 1) * C - k, :].rearrange("p c e -> p (c e)"), start=(k == 1),
                       stop=False, skip_group_check=True)
                mm(route_bank[b][:, 0:C * E], tri[:, :],
                   mask[:, b * C:(b + 1) * C, :].rearrange("p c e -> p (c e)"),
                   start=False, stop=True, skip_group_check=True).then_inc(posP, 1)

            def slot_rows(b):
                pe.wait_ge(pl, 6 * b + 6)
                for c in range(C):
                    last = mm(route_bank[b][:, c * P:(c + 1) * P],
                              slot_r[:, b * C + c:b * C + c + 1].broadcast_to([P, P]),
                              ident_r[:, :], start=True, stop=True)
                last.then_inc(srP, 1)

            def dispatch(b):
                for part in (x_hi, x_lo):
                    if part is x_hi:
                        pe.wait_ge(xhi, b + 1)
                    elif b < 2:
                        pe.wait_ge(xlo, b + 1)
                    else:
                        pe.wait_ge(xlv, b - 1)
                    for c in range(C):
                        if part is x_hi:
                            if c < DVE_HOT[b]:
                                pe.wait_ge(dsp, sum(DVE_HOT[:b]) + c + 1)
                            else:
                                pe.wait_ge(dspP, b * C - sum(DVE_HOT[:b]) + c - DVE_HOT[b] + 1)
                        last = mm(tok_bank[b][:, :], part[:, b * C + c, :], disp[:, b % 2, c, :],
                                  start=(c == 0 and part is x_hi), stop=(c == C - 1 and part is x_lo))
                last.then_inc(xeP, 1)

            pe.wait_ge(m_c, 3)
            pe.wait_ge(kv_c, 2)
            def wih_T():
                pe.wait_ge(wih_in, 16)
                for a in range(3):
                    last = tr(bank[1][:, a * P:(a + 1) * P], wih_t[:, a, :], ident[:, :])
                last.then_inc(wtr, 1)

            scores(0, 0)
            mean_squares(0, 0)
            wih_T()
            v_wih(0)
            pe.wait_ge(fold_set, 4)
            pe.wait_ge(m_c, 4)
            exp_sums(0, 0)
            v_wih(1)
            norm_T(2)
            denominators(0, 0)
            norm_T(3)
            v_wih(2)
            pe.wait_ge(wtr_c, 3)
            slots_r(0, 0, 0)
            pe.wait_ge(pick_set, 5)
            four_sets(0, 0, 0)
            pe.wait_ge(wtr_c, 4)
            pe.wait_ge(vw_c, 1)
            slots_z(0, 0, 0)
            pe.wait_ge(wtr_c, 3)
            pe.wait_ge(bn_set, 4)
            slots_n(0, 0, 0)
            x_T(2)
            pe.wait_ge(vw_c, 1)
            attn_r(0, 0, 0)
            x_T(3)
            pe.wait_ge(xTc, 3)
            mean_squares(1, 0)
            four_sets(0, 1, 0)
            pe.wait_ge(vw_c, 1)
            attn_z(0, 0, 0)
            pe.wait_ge(xTc, 4)
            scores(1, 0)
            pe.wait_ge(vw_c, 1)
            attn_n(0, 0, 0)
            v_wih(3)
            slots_r(0, 1, 0)
            pe.wait_ge(vw_c, 2)
            attn_r(0, 1, 0)
            slots_z(0, 1, 0)
            slots_n(0, 1, 0)
            pe.wait_ge(vw_c, 2)
            attn_z(0, 1, 0)
            pe.wait_ge(vw_c, 2)
            attn_n(0, 1, 0)
            pe.wait_ge(vw_c, B)
            exp_sums(1, 0)
            denominators(1, 0)
            slots_z(1, 0, 0)
            slots_n(1, 0, 0)
            four_sets(1, 0, 0)
            slots_r(1, 0, 0)
            for half in range(1, HALVES - 1):
                t, g = divmod(half, NG)
                ot, og = divmod(half + 1, NG)
                attn_r(g, 0, t)
                attn_z(g, 0, t)
                mean_squares(og, ot)
                four_sets(g, 1, t)
                scores(og, ot)
                attn_n(g, 0, t)
                slots_r(g, 1, t)
                slots_z(g, 1, t)
                attn_r(g, 1, t)
                slots_n(g, 1, t)
                attn_z(g, 1, t)
                exp_sums(og, ot)
                attn_n(g, 1, t)
                denominators(og, ot)
                slots_r(og, 0, ot)
                slots_z(og, 0, ot)
                slots_n(og, 0, ot)
                four_sets(og, 0, ot)
            t, g = ITERS - 1, NG - 1
            attn_r(g, 0, t)
            attn_z(g, 0, t)
            four_sets(g, 1, t)
            x2_back(0)
            logits(0)
            x2_back(1)
            attn_n(g, 0, t)
            slots_n(g, 1, t)
            slots_r(g, 1, t)
            logits(1)
            attn_r(g, 1, t)
            slots_z(g, 1, t)
            attn_z(g, 1, t)
            attn_n(g, 1, t)
            x2_back(2)
            positions(0)
            positions(1)
            slot_rows(0)
            logits(2)
            slot_rows(1)
            dispatch(0)
            x2_back(3)
            logits(3)
            positions(2)
            dispatch(1)
            positions(3)
            slot_rows(2)
            dispatch(2)
            dispatch(3)
            slot_rows(3)

            def up(k):
                for e in range(2):
                    ex_ = 2 * k + e
                    rhs = xe[:, ex_, :, :].rearrange("p b c -> p (b c)")
                    for half in range(2):
                        n = 2 * ex_ + half
                        if n >= 2:
                            pe.wait_ge(hidC, n - 1)
                        for a in range(2):
                            j = 2 * half + a
                            last = mm(hid_bank[half][:, a * B * CAP:(a + 1) * B * CAP],
                                      W1_t[:, ex_, j * P:(j + 1) * P], rhs, start=True, stop=True)
                        last.then_inc(hidP, 1)

            def down(k):
                if k == 0:
                    pe.wait_ge(srC, B)
                pe.wait_ge(hidC, 4 * (k + 1))
                if k >= 2:
                    pe.wait_ge(yl, k - 1)
                for b in range(B):
                    for j in range(J):
                        for e in range(2):
                            last = mm(y_bank[k % 2][e * CAP:(e + 1) * CAP, b * D:(b + 1) * D],
                                      hid[k % 2][:, e, j, b * CAP:(b + 1) * CAP], W2_t[:, 2 * k + e, j, :],
                                      start=(j == 0), stop=(j == J - 1))
                last.then_inc(yP, 1)

            def combine_batch(k, b):
                pe.wait_ge(yl, k + 1)
                pe.wait_ge(cmb, k * B + b + 1)
                for part in (y_hi, y_lo):
                    last = mm(tok_bank[b][:, :], part[:, k % 2, b, :], comb[k % 2][:, b, :],
                              start=(k == 0 and part is y_hi), stop=(k == NP - 1 and part is y_lo))
                if k == NP - 1 or b == B - 1:
                    last.then_inc(accP, 1)

            pe.wait_ge(w1_in, 16)
            pe.wait_ge(w2_in, 16)
            pe.wait_ge(xeC, B)
            pe.wait_ge(srC, 2)
            up(0)
            for k in range(NP):
                if k + 1 < NP:
                    up(k + 1)
                down(k)
                if k > 0:
                    for b in range(B):
                        combine_batch(k - 1, b)

            def back(b):
                pe.wait_ge(oTs, b + 1)
                for c in range(C):
                    last = tr(back_bank[b][:, c * P:(c + 1) * P], oT[:, b, c * P:(c + 1) * P], ident[:, :])
                last.then_inc(backP, 1)

            combine_batch(NP - 1, 0)
            combine_batch(NP - 1, 1)
            for b in range(B):
                if b + 2 < B:
                    combine_batch(NP - 1, b + 2)
                back(b)


_INS = ["x", "ctx_1024", "L0_xattn_Wq", "L0_xattn_Wk", "L0_xattn_Wv", "L0_xattn_gru_wih", "L0_xattn_gru_whh",
        "L0_xattn_gru_bih", "L0_xattn_gru_bhh", "L0_xattn_slot_norm_w", "L0_xattn_input_norm_w",
        "L0_ffn_Wg", "L0_ffn_W1", "L0_ffn_W2"]


def kernel(**inputs):
    import numpy as _np
    import concourse.bacc as _bacc
    from concourse import mybir as _mybir
    from concourse.bass_utils import run_bass_kernel_spmd as _run

    nc = _bacc.Bacc("TRN2", target_bir_lowering=False, num_devices=1)
    arrays, args = {}, []
    for name in _INS:
        a = _np.ascontiguousarray(inputs[name])
        arrays[f"in_{name}_dram"] = a
        args.append(nc.dram_tensor(f"in_{name}_dram", a.shape, _mybir.dt.from_np(a.dtype), kind="ExternalInput").ap())
    shape = tuple(inputs["x"].shape)
    args.append(nc.dram_tensor("out_0_dram", shape, _mybir.dt.float32, kind="ExternalOutput").ap())
    slot_attention_and_switch_ffn(nc, *args)
    r = _run(nc, [arrays], core_ids=[0])
    return r.results[0]["out_0_dram"]
```
